# Optimizing a Trainium2 kernel written in Bass

```python
import numpy as np
import jax
import jax.numpy as jnp

def _softmax(x, axis=-1):
    return jax.nn.softmax(x, axis=axis)

def _gelu(x):
    return jax.nn.gelu(x, approximate=True)

def _silu(x):
    return jax.nn.silu(x)

def _sigmoid(x):
    return jax.nn.sigmoid(x)

def _layernorm(x, axis=-1, eps=1e-05):
    m = jnp.mean(x, axis=axis, keepdims=True)
    v = jnp.var(x, axis=axis, keepdims=True)
    return (x - m) / jnp.sqrt(v + eps)

def _scatter_add(tgt, idx, src, axis=0):
    return tgt.at[idx].add(src)

def _segment_sum(src, seg, n):
    return jax.ops.segment_sum(src, seg, n)
kernel_name = 'mk_vit_tower_cls_d1_tok_img768_r4_34ed23'

def setup_inputs(seed: int=0):
    np.random.seed(seed)
    _w = jnp.asarray

    def _rec_inputs():
        import jax
        import jax.numpy as jnp
        _rk = jax.random.key(seed)
        x = -0.00016672 + 0.999947 * jax.random.normal(jax.random.fold_in(_rk, 1), (16, 128, 128, 3), jnp.float32)
        cls_tok = 0.02 * jax.random.normal(jax.random.fold_in(_rk, 5), (1, 1, 192), jnp.float32)
        return (x, cls_tok)
    x, cls_tok = _rec_inputs()

    def _L0_tok_setup():
        import jax, jax.numpy as jnp
        import numpy as np
        PATCH = 16
        D_MODEL = 192

        def _patchify(imgs, p):
            B, H, Wd, C = imgs.shape
            nh, nw = (H // p, Wd // p)
            x = imgs.reshape(B, nh, p, nw, p, C)
            x = x.transpose(0, 1, 3, 2, 4, 5)
            return x.reshape(B, nh * nw, p * p * C)
        key = jax.random.key(seed)
        k1, k2 = jax.random.split(key)
        B, H, W_, C = (64, 96, 96, 3)
        imgs = jax.random.normal(k1, (B, H, W_, C), dtype=jnp.float32)
        patch_dim = PATCH * PATCH * C
        W = jax.random.normal(k2, (patch_dim, D_MODEL), dtype=jnp.float32) * (1.0 / np.sqrt(patch_dim))
        b = jnp.zeros((D_MODEL,), dtype=jnp.float32)
        return {'imgs': imgs, 'W': W, 'b': b}
    _L0_tok_all = _L0_tok_setup()
    _L0_tok_in = {k: v for k, v in _L0_tok_all.items() if k in ('W', 'b')}
    del _L0_tok_all

    def _L0_attn_setup():
        import jax, jax.numpy as jnp
        import numpy as np
        D_IN = 192
        N_HEADS = 12
        HEAD_DIM = 192 // N_HEADS
        B, S = (4, 512)
        key = jax.random.key(seed)
        ks = jax.random.split(key, 10)
        sc = 0.02
        x = jax.random.normal(ks[0], (B, S, D_IN), dtype=jnp.float32)
        Wq = jax.random.normal(ks[1], (N_HEADS, D_IN, HEAD_DIM), dtype=jnp.float32) * sc
        Wk = jax.random.normal(ks[2], (N_HEADS, D_IN, HEAD_DIM), dtype=jnp.float32) * sc
        Wv = jax.random.normal(ks[3], (N_HEADS, D_IN, HEAD_DIM), dtype=jnp.float32) * sc
        bq = jax.random.normal(ks[4], (N_HEADS, HEAD_DIM), dtype=jnp.float32) * sc
        bk = jax.random.normal(ks[5], (N_HEADS, HEAD_DIM), dtype=jnp.float32) * sc
        bv = jax.random.normal(ks[6], (N_HEADS, HEAD_DIM), dtype=jnp.float32) * sc
        Wo = jax.random.normal(ks[7], (N_HEADS * HEAD_DIM, N_HEADS * HEAD_DIM), dtype=jnp.float32) * sc
        bo = jax.random.normal(ks[8], (N_HEADS * HEAD_DIM,), dtype=jnp.float32) * sc
        return {'x': x, 'Wq': Wq, 'Wk': Wk, 'Wv': Wv, 'bq': bq, 'bk': bk, 'bv': bv, 'Wo': Wo, 'bo': bo}
    _L0_attn_all = _L0_attn_setup()
    _L0_attn_in = {k: v for k, v in _L0_attn_all.items() if k in ('Wq', 'Wk', 'Wv', 'bq', 'bk', 'bv', 'Wo', 'bo')}
    del _L0_attn_all

    def _L0_ffn_setup():
        import jax, jax.numpy as jnp
        import numpy as np
        EPS = 1e-06

        def l2_normalize(x, axis):
            norm = jnp.sqrt(jnp.square(x).sum(axis=axis, keepdims=True))
            return x * (1.0 / (norm + EPS))
        key = jax.random.key(seed)
        ks = jax.random.split(key, 8)
        b, m, d = (32, 256, 192)
        n, p = (8, 4)
        h = d // 8
        X = jax.random.normal(ks[0], (b, m, d), dtype=jnp.float32)
        std_slot = float(np.sqrt(2.0 / (d + n * p)))
        slot_params = jax.random.normal(ks[1], (d, n, p), dtype=jnp.float32) * std_slot
        scale = jnp.ones((), dtype=jnp.float32)
        W_down = jax.random.normal(ks[2], (n, d, h), dtype=jnp.float32) * float(np.sqrt(1.0 / d))
        b_down = jnp.zeros((n, h), dtype=jnp.float32)
        W_up = jax.random.normal(ks[3], (n, h, d), dtype=jnp.float32) * float(np.sqrt(1.0 / h))
        b_up = jnp.zeros((n, d), dtype=jnp.float32)
        return {'X': X, 'slot_params': slot_params, 'scale': scale, 'W_down': W_down, 'b_down': b_down, 'W_up': W_up, 'b_up': b_up}
    _L0_ffn_all = _L0_ffn_setup()
    _L0_ffn_in = {k: v for k, v in _L0_ffn_all.items() if k in ('slot_params', 'scale', 'W_down', 'b_down', 'W_up', 'b_up')}
    del _L0_ffn_all
    return {'x': x, 'cls_tok': cls_tok, 'L0_tok_W': _L0_tok_in['W'], 'L0_tok_b': _L0_tok_in['b'], 'L0_attn_Wq': _L0_attn_in['Wq'], 'L0_attn_Wk': _L0_attn_in['Wk'], 'L0_attn_Wv': _L0_attn_in['Wv'], 'L0_attn_bq': _L0_attn_in['bq'], 'L0_attn_bk': _L0_attn_in['bk'], 'L0_attn_bv': _L0_attn_in['bv'], 'L0_attn_Wo': _L0_attn_in['Wo'], 'L0_attn_bo': _L0_attn_in['bo'], 'L0_ffn_slot_params': _L0_ffn_in['slot_params'], 'L0_ffn_scale': _L0_ffn_in['scale'], 'L0_ffn_W_down': _L0_ffn_in['W_down'], 'L0_ffn_b_down': _L0_ffn_in['b_down'], 'L0_ffn_W_up': _L0_ffn_in['W_up'], 'L0_ffn_b_up': _L0_ffn_in['b_up']}

def reference(x, cls_tok, L0_tok_W, L0_tok_b, L0_attn_Wq, L0_attn_Wk, L0_attn_Wv, L0_attn_bq, L0_attn_bk, L0_attn_bv, L0_attn_Wo, L0_attn_bo, L0_ffn_slot_params, L0_ffn_scale, L0_ffn_W_down, L0_ffn_b_down, L0_ffn_W_up, L0_ffn_b_up):
    import jax
    import jax.numpy as jnp

    def _L0_tok_ref(imgs, W, b):
        import jax, jax.numpy as jnp
        import numpy as np
        PATCH = 16
        D_MODEL = 192

        def _patchify(imgs, p):
            B, H, Wd, C = imgs.shape
            nh, nw = (H // p, Wd // p)
            x = imgs.reshape(B, nh, p, nw, p, C)
            x = x.transpose(0, 1, 3, 2, 4, 5)
            return x.reshape(B, nh * nw, p * p * C)
        x = _patchify(imgs, PATCH)
        return jnp.einsum('bnd,de->bne', x, W) + b

    def _L0_attn_ref(x, Wq, Wk, Wv, bq, bk, bv, Wo, bo):
        import jax, jax.numpy as jnp
        import numpy as np
        D_IN = 192
        N_HEADS = 12
        HEAD_DIM = 192 // N_HEADS
        B, S = (4, 512)
        b, n, _ = x.shape
        q = jnp.einsum('bnd,hdk->bhnk', x, Wq) + bq[None, :, None, :]
        k = jnp.einsum('bnd,hdk->bhnk', x, Wk) + bk[None, :, None, :]
        v = jnp.einsum('bnd,hdk->bhnk', x, Wv) + bv[None, :, None, :]
        scores = jnp.einsum('bhqk,bhsk->bhqs', q, k)
        causal = jnp.tril(jnp.ones((n, n), dtype=bool))
        scores = jnp.where(causal[None, None, :, :], scores, -jnp.inf)
        scale = 1.0 / jnp.sqrt(jnp.asarray(HEAD_DIM, dtype=scores.dtype))
        weights = jax.nn.softmax(scores * scale, axis=-1)
        ctx = jnp.einsum('bhqs,bhsk->bhqk', weights, v)
        ctx = ctx.transpose(0, 2, 1, 3).reshape(b, n, N_HEADS * HEAD_DIM)
        return ctx @ Wo + bo

    def _L0_ffn_ref(X, slot_params, scale, W_down, b_down, W_up, b_up):
        import jax, jax.numpy as jnp
        import numpy as np
        EPS = 1e-06

        def l2_normalize(x, axis):
            norm = jnp.sqrt(jnp.square(x).sum(axis=axis, keepdims=True))
            return x * (1.0 / (norm + EPS))
        b, m, d = X.shape
        _, n, p = slot_params.shape
        Xn = l2_normalize(X, axis=-1)
        sp = l2_normalize(slot_params, axis=1) * scale
        logits = jnp.einsum('bmd,dnp->bmnp', Xn, sp)
        D = jax.nn.softmax(logits, axis=1)
        C = jax.nn.softmax(logits.reshape(b, m, n * p), axis=2).reshape(b, m, n, p)
        X_tilde = jnp.einsum('bmd,bmnp->bnpd', Xn, D)
        H = jax.nn.gelu(jnp.einsum('bnpd,ndh->bnph', X_tilde, W_down) + b_down[None, :, None, :], approximate=False)
        Y_tilde = jnp.einsum('bnph,nhd->bnpd', H, W_up) + b_up[None, :, None, :]
        Y = jnp.einsum('bnpd,bmnp->bmd', Y_tilde, C)
        return Y
    h = _L0_tok_ref(x, L0_tok_W, L0_tok_b)
    h = jnp.concatenate([jnp.broadcast_to(cls_tok, (h.shape[0], 1, h.shape[2])), h], axis=1)
    h = h + _L0_attn_ref(_layernorm(h, axis=-1), L0_attn_Wq, L0_attn_Wk, L0_attn_Wv, L0_attn_bq, L0_attn_bk, L0_attn_bv, L0_attn_Wo, L0_attn_bo)
    h = h + _L0_ffn_ref(_layernorm(h, axis=-1), L0_ffn_slot_params, L0_ffn_scale, L0_ffn_W_down, L0_ffn_b_down, L0_ffn_W_up, L0_ffn_b_up)
    return h

_drawn_inputs = setup_inputs


def setup_inputs(seed=0):
    import zlib

    import numpy as np

    out = dict(_drawn_inputs(seed))
    spreads = {'L0_tok_b': (0.0, 0.1), 'L0_ffn_b_down': (0.0, 0.419), 'L0_ffn_b_up': (0.0, 0.1)}
    factors = {'cls_tok': 4.011,
     'L0_attn_Wq': 8.0,
     'L0_attn_Wk': 8.0,
     'L0_attn_bq': 62.227,
     'L0_attn_bk': 64.0,
     'L0_attn_bv': 8.0,
     'L0_attn_bo': 2.668,
     'L0_ffn_slot_params': 8.0,
     'L0_ffn_W_down': 8.0,
     'L0_ffn_W_up': 2.984}
    for name, (base, spread) in spreads.items():
        noise = np.random.default_rng([zlib.crc32(name.encode()), seed]).standard_normal(out[name].shape)
        drawn = base * np.exp(spread * noise) if base else spread * noise
        out[name] = jnp.asarray(drawn.astype(out[name].dtype))
    for name, factor in factors.items():
        out[name] = (out[name] * factor).astype(out[name].dtype)
    return out
```

```python
from contextlib import ExitStack

import concourse.bass as bass
from concourse import mybir

F32 = mybir.dt.float32
BF16 = mybir.dt.bfloat16
ALU = mybir.AluOpType
ACT = mybir.ActivationFunctionType
AX = mybir.AxisListType

B, NPATCH, D, PIX = 16, 64, 192, 768
HEADS, HD = 12, 16
TOK = NPATCH + 1
EXPERTS, SLOTS, HID = 8, 4, 24
NS = EXPERTS * SLOTS
PAIRS = B // 2
KC = 2
DC = D // KC
PC = PIX // 128
HC = HEADS // KC
HP = HEADS // 2
VW = 2 * HD + 2
QW = 32
NG = EXPERTS // 4
ACT_HEADS = 3
SM_SCALE = HD ** -0.5
LN_EPS = 1e-5
L2_EPS = 1e-6
MASKED = -1e30

FIELDS_A = [("cls", D), ("btok", D), ("bo", D), ("bv", D), ("bq", KC), ("bk", KC), ("scale", 1)]
FIELDS_B = [("wq", KC * D), ("wk", KC * D), ("wv", KC * D)]
FIELDS_C = [("wo", KC * D), ("slots", KC * NS), ("wdown", KC * EXPERTS * QW), ("wup", NG * D), ("bdown", NG), ("bup", D)]


def width(fields):
    return sum(n for _, n in fields)


def offsets(fields):
    at, out = 0, {}
    for name, n in fields:
        out[name] = (at, n)
        at += n
    return out


def vit_tower_kernel(nc, xt, wtok, pack_a, pack_b, pack_c, out):
    with ExitStack() as ctx:
        def sb(name, shape, dt=F32):
            return ctx.enter_context(nc.sbuf_tensor(name, shape, dt))

        def sem(name):
            return ctx.enter_context(nc.semaphore(name))

        ident = sb("ident", [128, 128])
        ident_b = sb("ident_b", [128, 128], BF16)
        causal = sb("causal", [128, HC, TOK], BF16)
        slot_mask = sb("slot_mask", [64, 129], BF16)
        head_mask = sb("head_mask", [DC, HC])
        cls_head_mask = sb("cls_head_mask", [HEADS, HP, VW])
        cls_row_mask = sb("cls_row_mask", [64, PAIRS, B])
        powers = sb("powers", [128, 3])
        halves = sb("halves", [DC, KC, SLOTS])

        wt = sb("wt", [128, PC, D])
        pa = sb("pa", [128, width(FIELDS_A)])
        pb = sb("pb", [DC, width(FIELDS_B)])
        pc = sb("pc", [128, width(FIELDS_C)])

        def field(name):
            for tile, fields in ((pa, FIELDS_A), (pb, FIELDS_B), (pc, FIELDS_C)):
                if name in offsets(fields):
                    a, n = offsets(fields)[name]
                    return tile[:, a:a + n]

        cls_in, b_tok, b_o, b_v = field("cls"), field("btok"), field("bo"), field("bv")
        b_q, b_k, slot_scale = field("bq"), field("bk"), field("scale")
        w_q = field("wq").rearrange("p (k n) -> p k n", k=KC)
        w_k = field("wk").rearrange("p (k n) -> p k n", k=KC)
        w_v = field("wv").rearrange("p (k n) -> p k n", k=KC)
        w_o = field("wo")[0:DC].rearrange("p (k n) -> p k n", k=KC)
        slots_in = field("slots")[0:DC].rearrange("p (k n) -> p k n", k=KC)
        w_down = field("wdown")[0:DC].rearrange("p (k e h) -> p k e h", k=KC, e=EXPERTS)
        w_up = field("wup").rearrange("p (g n) -> p g n", g=NG)
        b_down, b_up = field("bdown"), field("bup")

        slot_sq = sb("slot_sq", [DC, KC, NS])
        slot_ss = sb("slot_ss", [DC, KC, SLOTS])
        slot_inv = sb("slot_inv", [DC, KC, SLOTS])
        slot_dirs = sb("slot_dirs", [DC, KC, 2, NS])

        xt_first = sb("xt_first", [128, PC, 128])
        xt_next = sb("xt_next", [128, PC, 128])
        h_tok = sb("h_tok", [128, D])
        ln1_bn = sb("ln1_bn", [128, 6])
        ln1_mv = sb("ln1_mv", [128, 2])
        ln1_rstd = sb("ln1_rstd", [128, 2])
        ln1 = sb("ln1", [128, D])
        ln1_t = sb("ln1_t", [DC, KC, 2, TOK])
        q_t = sb("q_t", [DC, KC, 128])
        k_t = sb("k_t", [DC, KC, 2 * TOK])
        k_heads = sb("k_heads", [DC, KC, 2, HC, TOK])
        v_pairs = sb("v_pairs", [128, 2, HP, VW])
        s_max = sb("s_max", [128, HEADS])
        s_sub = sb("s_sub", [128, HEADS, TOK])
        probs = sb("probs", [128, HEADS, NPATCH])
        probs_cls = sb("probs_cls", [128, HEADS])
        probs_t = sb("probs_t", [128, HP, 128])
        probs_cls_t = sb("probs_cls_t", [HEADS, 128])
        p_inv = sb("p_inv", [128, HEADS])
        ctx_n = sb("ctx_n", [128, D])
        ctx_t = sb("ctx_t", [DC, KC, 128])
        ln2_bn = sb("ln2_bn", [128, 6])
        ln2_mv = sb("ln2_mv", [128, 2])
        ln2_s = sb("ln2_s", [128, 7])
        xn = sb("xn", [128, D])
        xn_t = sb("xn_t", [DC, KC, 129])
        c_max = sb("c_max", [128, 1])
        c_exp = sb("c_exp", [128, NS])
        c_sum = sb("c_sum", [128, 1])
        c_inv = sb("c_inv", [128, 1])
        comb = sb("comb", [128, 2, NS])
        d_max = sb("d_max", [64, 1])
        d_exp = sb("d_exp", [64, 129])
        d_sum = sb("d_sum", [64, 1])
        d_inv = sb("d_inv", [64, 1])
        disp = sb("disp", [64, 129])
        disp_t = sb("disp_t", [128, 64])
        disp_cls = sb("disp_cls", [64, 64])

        h_all = sb("h_all", [128, PAIRS, D])
        comb_t = sb("comb_t", [64, PAIRS, 128])
        slots_t = sb("slots_t", [DC, KC, B, NS])
        hidden = sb("hidden", [128, NG, B, EXPERTS, SLOTS])
        y_slots = sb("y_slots", [64, PAIRS, D])

        c_bn = sb("c_bn", [64, 6])
        c_mv = sb("c_mv", [64, 2])
        c_rstd = sb("c_rstd", [64, 2])
        cls_ln = sb("cls_ln", [64, D])
        cls_ln_t = sb("cls_ln_t", [DC, KC, 64])
        cls_v = sb("cls_v", [64, D])
        cls_v_heads = sb("cls_v_heads", [HEADS, HP, VW])
        cls_v_t = sb("cls_v_t", [DC, KC, 64])
        cls_h = sb("cls_h", [64, D])
        c2_bn = sb("c2_bn", [64, 6])
        c2_mv = sb("c2_mv", [64, 2])
        c2_s = sb("c2_s", [64, 7])
        cls_xn = sb("cls_xn", [64, D])
        cls_xn_t = sb("cls_xn_t", [DC, KC, 64])
        cc_max = sb("cc_max", [64, 1])
        cc_exp = sb("cc_exp", [64, NS])
        cc_sum = sb("cc_sum", [64, 1])
        cc_inv = sb("cc_inv", [64, 1])
        cc = sb("cc", [64, 2, NS])
        cls_comb_t = sb("cls_comb_t", [64, PAIRS, B])
        cls_out = sb("cls_out", [B, D])
        warm = sb("warm", [128, 1])

        bank = [ctx.enter_context(nc.psum_tensor(f"bank{i}", [128, 512], F32)) for i in (4, 5, 6, 7)]
        s_ps = ctx.enter_context(nc.psum_tensor("s_ps", [128, KC, 512], F32))
        pt_ps = ctx.enter_context(nc.psum_tensor("pt_ps", [128, 2, 512], F32))
        qx_ps, kl_ps, vm_ps, o_ps = bank
        cls_ps = pt_ps[:, 0, :]

        in_first, in_next, in_wt, in_a, in_b, in_c = (sem(n) for n in (
            "in_first", "in_next", "in_wt", "in_a", "in_b", "in_c"))
        const_a, hidden_zero, slot_step, cls_step = (sem(n) for n in ("const_a", "hidden_zero", "slot_step", "cls_step"))
        cls_col, cls_xn_col, slot_inv_ready = sem("cls_col"), sem("cls_xn_col"), sem("slot_inv_ready")
        (tok_done, ln1t_done, qk_done, v_done, s_done, pta_done, ptb_done, pv_done, ot_done, wo_done, xnt_done,
         ll_done, dc_done, xx_done) = (sem(n) for n in (
             "tok_done", "ln1t_done", "qk_done", "v_done", "s_done", "pta_done", "ptb_done", "pv_done", "ot_done",
             "wo_done", "xnt_done", "ll_done", "dc_done", "xx_done"))
        (h_ready, hbo_ready, ln1_step, ln1t_ready, q_ready, k_ready, km_act_ready, km_dve_ready, v_ready, smax_ready, ssub_ready,
         probs_ready, pta_ready, ptb_ready, pinv_ready, ctx_ready, ctxt_ready, h1_ready, ln2_step, xnt_ready,
         cmax_ready, cexp_ready, cinv_ready, comb_ready, dmax_ready, dexp_ready, dinv_ready, disp_ready,
         dcls_ready, dispt_ready, combt_ready, slots_ready) = (sem(n) for n in (
             "h_ready", "hbo_ready", "ln1_step", "ln1t_ready", "q_ready", "k_ready", "km_act_ready", "km_dve_ready",
             "v_ready",
             "smax_ready", "ssub_ready", "probs_ready", "pta_ready", "ptb_ready", "pinv_ready", "ctx_ready",
             "ctxt_ready", "h1_ready", "ln2_step", "xnt_ready", "cmax_ready", "cexp_ready", "cinv_ready",
             "comb_ready", "dmax_ready", "dexp_ready", "dinv_ready", "disp_ready", "dcls_ready", "dispt_ready",
             "combt_ready", "slots_ready"))
        passed = sem("passed")
        hid_done, hid_ready, ys_done, ys_ready, y_done, y_ready, yc_done, yc_ready, out_sp, out_act = (sem(n) for n in (
            "hid_done", "hid_ready", "ys_done", "ys_ready", "y_done", "y_ready", "yc_done", "yc_ready",
            "out_sp", "out_act"))
        SLOT_STEPS = 10
        IDENT, POWERS, HEAD_MASK, CAUSAL, CLS_HEADS, SLOT_MASK, CONSTANTS = 2, 5, 8, 12, 15, 18, 21
        LN1_STEPS, LN2_STEPS = 5, 7
        names = ("stats mean var_eps rstd ln ln_turned ln_t v_ps v v_heads v_turned v_t wo_ps h".split()
                 + [f"norm2_{i}" for i in range(1, LN2_STEPS)]
                 + "xn xn_turned xn_t logits max exp inv comb comb_turned comb_t".split())
        CLS = {name: i + 1 for i, name in enumerate(names)}

        def has(eng, s, n):
            if not isinstance(n, int) or n > 0:
                eng.wait_ge(s, n)

        def settled(eng):
            eng.sem_inc(passed, 1)

        def capped(n):
            return min(n, PAIRS) if isinstance(n, int) else n

        def all_slots(eng, run):
            def peeled(first, end):
                for t in range(first, end):
                    run(t, lambda k: 0 <= t + k < PAIRS)

            peeled(-2, 2)
            with eng.Fori(2, PAIRS - 2) as t:
                run(t, lambda k: True)
            peeled(PAIRS - 2, PAIRS + 1)

        block = ctx.enter_context(nc.Block())

        @block.sync
        def _(sp):
            sp.dma_start(wt[:, :, :], wtok).then_inc(in_wt, 16)
            sp.dma_start(xt_first[:, :, :], xt[0]).then_inc(in_first, 16)
            sp.dma_start(pb[:, :], pack_b).then_inc(in_b, 16)
            sp.dma_start(xt_next[:, :, :], xt[1]).then_inc(in_next, 16)
            sp.dma_start(pc[:, :], pack_c).then_inc(in_c, 16)
            with sp.Fori(2, PAIRS) as p:
                sp.wait_ge(tok_done, p)
                sp.dma_start(xt_next[:, :, :], xt[p]).then_inc(in_next, 16)
            for p in range(PAIRS):
                sp.wait_ge(y_ready, p + 1)
                sp.dma_start(out[2 * p, 1:TOK, :], h_all[0:64, p, :]).then_inc(out_sp, 16)
            sp.wait_ge(yc_ready, 1)
            sp.dma_start(out[:, 0, :], cls_out[:, :]).then_inc(out_sp, 16)
            sp.wait_ge(out_sp, 16 * (PAIRS + 1))

        @block.gpsimd
        def _(pool):
            made = [0]

            def then(instruction):
                made[0] += 1
                instruction.then_inc(const_a, 1)
                pool.wait_ge(const_a, made[0])

            def keep(tile, compare, fill, base, pattern, channel):
                then(pool.affine_select(out=tile, in_=tile, compare_op=compare, fill=fill, base=base,
                                        pattern=pattern, channel_multiplier=channel))

            then(pool.memset(ident[:, :], 0.0))
            keep(ident[:, :], ALU.not_equal, 1.0, 0, [[-1, 128]], 1)
            then(pool.memset(powers[:, 0:1], -0.5))
            then(pool.memset(powers[:, 1:3], 0.5))
            then(pool.memset(halves[:, :, :], 0.5))
            then(pool.memset(head_mask[:, :], 1.0))
            keep(head_mask[:, :], ALU.is_ge, 0.0, 0, [[-HD, HC]], 1)
            keep(head_mask[:, :], ALU.is_ge, 0.0, HD - 1, [[HD, HC]], -1)
            then(pool.tensor_copy(ident_b[:, :], ident[:, :]))
            then(pool.memset(causal[:, :, :], 0.0))
            for b in range(2):
                keep(causal[64 * b:64 * b + 64], ALU.is_ge, MASKED, 1, [[0, HC], [-1, TOK]], 1)
            then(pool.memset(cls_head_mask[:, :, :], 1.0))
            keep(cls_head_mask[:, :, 0:2 * HD].rearrange("h p (e d) -> h p e d", e=2), ALU.is_equal, 0.0, 0,
                 [[-2, HP], [-1, 2], [0, HD]], 1)
            keep(cls_head_mask[:, :, 2 * HD:VW], ALU.is_equal, 0.0, 0, [[-2, HP], [-1, 2]], 1)
            then(pool.memset(slot_mask[:, :], 0.0))
            for b in range(2):
                then(pool.memset(slot_mask[NS * b:NS * b + NS, 64 * (1 - b):64 * (1 - b) + 64], MASKED))
            then(pool.memset(cls_row_mask[:, :, :], 1.0))
            for b in range(2):
                keep(cls_row_mask[NS * b:NS * b + NS], ALU.is_equal, 0.0, -b, [[-2, PAIRS], [1, B]], 0)
            assert made[0] == CONSTANTS

            def power(dst, src, exponents, step, n):
                pool.wait_ge(step, n)
                pool.tensor_tensor(dst, src, exponents, ALU.pow).then_inc(step, 1)

            def slot(t, there):
                early = isinstance(t, int)
                if early and t == -2:
                    power(c_rstd[:, 1:2], c_rstd[:, 0:1], powers[0:64, 0:1], cls_step, CLS["var_eps"])
                if early and t == -1:
                    power(slot_ss[:, :, :], slot_ss[:, :, :], halves[:, :, :], slot_step, 6)
                if there(-1):
                    power(ln2_s[:, 2:4], ln2_s[:, 0:2], powers[:, 1:3], ln2_step, LN2_STEPS * (t - 1) + 3)
                if there(2):
                    p = t + 2
                    power(ln1_rstd[:, 1:2], ln1_rstd[:, 0:1], powers[:, 0:1], ln1_step, LN1_STEPS * p + 3)
                    if early and p == 0:
                        pool.wait_ge(in_a, 16)
                    pool.wait_ge(h_ready, p + 1)
                    pool.tensor_tensor(h_all[:, p, :], h_tok[:, :], b_o, ALU.add).then_inc(hbo_ready, 1)
                if early and t == -1:
                    power(c2_s[:, 2:4], c2_s[:, 0:2], powers[0:64, 1:3], cls_step, CLS["norm2_3"])
                if there(-1):
                    p = t - 1
                    pool.wait_ge(disp_ready, p + 1)
                    has(pool, xx_done, p)
                    settled(pool)
                    pool.tensor_scalar(disp_cls[:, :], ident[0:64, 0:64], disp[:, 128:129], None,
                                       ALU.mult).then_inc(dcls_ready, 1)

            all_slots(pool, slot)

        @block.tensor
        def _(pe):
            mm, tr = pe.matmul, pe.transpose

            def two_transposes(dst, src, rows):
                for kc in range(KC):
                    last = tr(dst[0:DC, kc * rows:(kc + 1) * rows], src[0:rows, kc * DC:(kc + 1) * DC],
                              ident[0:rows, 0:rows])
                return last

            def two_chunks(dst, lhs, rhs, first=True):
                for kc in range(KC):
                    last = mm(dst, lhs(kc), rhs(kc), start=first and kc == 0, stop=kc == KC - 1)
                return last

            def cls_part(result):
                if result == "ln_turned":
                    pe.wait_ge(cls_step, CLS["ln"])
                    two_transposes(cls_ps, cls_ln, 64).then_inc(cls_step, 1)
                if result == "v_ps":
                    pe.wait_ge(in_b, 16)
                    pe.wait_ge(cls_step, CLS["ln_t"])
                    two_chunks(cls_ps[0:64, 0:D], lambda k: cls_ln_t[:, k, :], lambda k: w_v[:, k, :])\
                        .then_inc(cls_step, 1)
                if result == "v_turned":
                    pe.wait_ge(cls_step, CLS["v_heads"])
                    two_transposes(cls_ps, cls_v, 64).then_inc(cls_step, 1)
                if result == "wo_ps":
                    pe.wait_ge(in_c, 16)
                    pe.wait_ge(cls_step, CLS["v_t"])
                    two_chunks(cls_ps[0:64, 0:D], lambda k: cls_v_t[:, k, :], lambda k: w_o[:, k, :])\
                        .then_inc(cls_step, 1)
                if result == "xn_turned":
                    pe.wait_ge(cls_step, CLS["xn"])
                    two_transposes(cls_ps, cls_xn, 64).then_inc(cls_step, 1)
                if result == "logits":
                    pe.wait_ge(cls_step, CLS["xn_t"])
                    pe.wait_ge(slot_step, SLOT_STEPS)
                    two_chunks(cls_ps[0:64, 0:NS], lambda k: cls_xn_t[:, k, :], lambda k: slot_dirs[:, k, 0, :])\
                        .then_inc(cls_step, 1)
                if result == "comb_turned":
                    pe.wait_ge(cls_step, CLS["comb"])
                    tr(cls_ps[0:64, 0:64], cc[:, :, :].rearrange("p b s -> p (b s)"), ident[0:64, 0:64])\
                        .then_inc(cls_step, 1)

            def slot(t, there):
                early = isinstance(t, int)
                if there(1):
                    p = t + 1
                    pe.wait_ge(ln1t_ready, p + 1)
                    has(pe, combt_ready, p - 2)
                    has(pe, dispt_ready, p - 2)
                    has(pe, ctxt_ready, p - 1)
                    for m in range(KC):
                        q_rhs = lambda k: ln1_t[:, k, :, 1:TOK]
                        k_rhs = lambda k: ln1_t[:, k, :, :]
                        two_chunks(qx_ps[0:DC, m * 128:(m + 1) * 128],
                                   lambda k: w_q[:, k, m * DC:(m + 1) * DC], q_rhs)
                        last = two_chunks(kl_ps[0:DC, m * 2 * TOK:(m + 1) * 2 * TOK],
                                          lambda k: w_k[:, k, m * DC:(m + 1) * DC], k_rhs)
                    last.then_inc(qk_done, 1)
                if early and t == -1:
                    cls_part("v_turned")
                if there(2):
                    p = t + 2
                    if early and p == 0:
                        pe.wait_ge(in_wt, 16)
                        pe.wait_ge(in_first, 16)
                    else:
                        pe.wait_ge(in_next, 16 * p)
                    has(pe, slots_ready, p - 3)
                    has(pe, v_ready, p - 1)
                    x = xt_first if early and p == 0 else xt_next
                    for c in range(PC):
                        last = mm(vm_ps[:, 0:D], x[:, c, :], wt[:, c, :], start=c == 0, stop=c == PC - 1)
                    last.then_inc(tok_done, 1)
                if early and t == -2:
                    pe.wait_ge(const_a, IDENT)
                    cls_part("ln_turned")
                    cls_part("v_ps")
                if early and t == -1:
                    cls_part("wo_ps")
                if early and t == 0:
                    cls_part("xn_turned")
                if there(-1):
                    p = t - 1
                    pe.wait_ge(ln2_step, LN2_STEPS * (p + 1))
                    has(pe, q_ready, capped(p + 3))
                    two_transposes(qx_ps, xn, 128).then_inc(xnt_done, 1)
                if early and t == 0:
                    cls_part("logits")
                    cls_part("comb_turned")
                if there(0):
                    p = t
                    if early and p == 0:
                        pe.wait_ge(cls_step, CLS["comb_t"])
                    pe.wait_ge(probs_ready, p + 1)
                    has(pe, pta_ready, p)
                    for i in range(4):
                        last = tr(pt_ps[:, 0, i * 128:(i + 1) * 128], probs[:, 2 * i:2 * i + 2, :].rearrange("p h j -> p (h j)"), ident[:, :])
                    last.then_inc(pta_done, 1)
                    has(pe, ptb_ready, p)
                    for i in range(4, HP):
                        tr(pt_ps[:, 1, (i - 4) * 128:(i - 3) * 128], probs[:, 2 * i:2 * i + 2, :].rearrange("p h j -> p (h j)"), ident[:, :])
                    tr(pt_ps[0:HEADS, 1, 256:384], probs_cls[:, :], ident[:, :]).then_inc(ptb_done, 1)
                if there(-1):
                    p = t - 1
                    pe.wait_ge(xnt_ready, p + 1)
                    has(pe, k_ready, capped(p + 3))
                    if early and p == 0:
                        pe.wait_ge(cls_xn_col, 1)
                        pe.wait_ge(const_a, SLOT_MASK)
                    two_chunks(kl_ps[:, 0:NS], lambda k: xn_t[:, k, 0:128], lambda k: slot_dirs[:, k, 0, :])
                    mm(kl_ps[0:64, 64:64 + 129], ident_b[0:64, 0:64], slot_mask[:, :], start=True, stop=False)
                    two_chunks(kl_ps[0:64, 64:64 + 129],
                               lambda k: slot_dirs[:, k, :, :].rearrange("p b s -> p (b s)"),
                               lambda k: xn_t[:, k, :], first=False).then_inc(ll_done, 1)
                if there(0):
                    p = t
                    has(pe, h1_ready, p)
                    pe.wait_ge(pta_ready, p + 1)
                    pe.wait_ge(ptb_ready, p + 1)
                    pe.wait_ge(v_ready, p + 1)
                    mm(o_ps[:, 0:HP * VW], probs_cls_t[:, :], cls_v_heads[:, :, :].rearrange("h p w -> h (p w)"),
                       start=True, stop=False, skip_group_check=True)
                    for i in range(HP):
                        for b in range(2):
                            last = mm(o_ps[64 * b:64 * b + 64, i * VW:(i + 1) * VW],
                                      probs_t[:, i, 64 * b:64 * b + 64], v_pairs[:, b, i, :],
                                      start=False, stop=True, skip_group_check=True)
                    last.then_inc(pv_done, 1)
                if there(1):
                    p = t + 1
                    has(pe, h_ready, capped(p + 2))
                    two_chunks(vm_ps[0:64, 0:D], lambda k: ln1_t[:, k, 0, 1:TOK], lambda k: w_v[:, k, :])
                    two_chunks(vm_ps[64:128, 0:D], lambda k: ln1_t[:, k, 1, 1:TOK], lambda k: w_v[:, k, :])\
                        .then_inc(v_done, 1)

                def scores(m):
                    p = t + 1
                    if m == 0:
                        if early and p == 0:
                            pe.wait_ge(const_a, CAUSAL)
                        has(pe, ssub_ready, p)
                        pe.wait_ge(q_ready, p + 1)
                        pe.wait_ge(km_act_ready, p + 1)
                        pe.wait_ge(km_dve_ready, p + 1)
                    dst = s_ps[:, m, 0:HC * TOK]
                    mm(dst, ident_b[:, :], causal[:, :, :].rearrange("p h j -> p (h j)"), start=True, stop=False,
                       skip_group_check=True)
                    for b in range(2):
                        last = mm(s_ps[64 * b:64 * b + 64, m, 0:HC * TOK], q_t[:, m, 64 * b:64 * b + 64],
                                  k_heads[:, m, b, :, :].rearrange("d h j -> d (h j)"), start=False, stop=True,
                                  skip_group_check=True)
                    if m == KC - 1:
                        last.then_inc(s_done, 1)

                if there(1):
                    scores(0)
                if there(-1):
                    p = t - 1
                    pe.wait_ge(disp_ready, p + 1)
                    pe.wait_ge(comb_ready, p + 1)
                    settled(pe)
                    tr(qx_ps[0:64, 128:256], comb[:, :, :].rearrange("p b s -> p (b s)"), ident[:, :])
                    tr(qx_ps[:, 0:64], disp[:, 0:128], ident[0:64, 0:64]).then_inc(dc_done, 1)
                if there(0):
                    p = t
                    pe.wait_ge(ctx_ready, p + 1)
                    has(pe, cexp_ready, p)
                    has(pe, dexp_ready, p)
                    two_transposes(kl_ps, ctx_n, 128).then_inc(ot_done, 1)
                if there(1):
                    scores(1)
                if there(2):
                    p = t + 2
                    pe.wait_ge(ln1_step, LN1_STEPS * (p + 1))
                    has(pe, ctx_ready, p - 1)
                    two_transposes(o_ps, ln1, 128).then_inc(ln1t_done, 1)
                if there(-1):
                    p = t - 1
                    pe.wait_ge(dispt_ready, p + 1)
                    pe.wait_ge(dcls_ready, p + 1)
                    has(pe, v_ready, capped(p + 3))
                    for kc in range(KC):
                        mm(vm_ps[0:DC, kc * 64:(kc + 1) * 64], xn[:, kc * DC:(kc + 1) * DC], disp_t[:, :],
                           start=True, stop=False)
                        last = mm(vm_ps[0:DC, kc * 64:(kc + 1) * 64], cls_xn[:, kc * DC:(kc + 1) * DC],
                                  disp_cls[:, :], start=False, stop=True)
                    last.then_inc(xx_done, 1)
                if there(0):
                    p = t
                    pe.wait_ge(ctxt_ready, p + 1)
                    has(pe, ln1t_ready, capped(p + 3))
                    two_chunks(o_ps[:, 0:D], lambda k: ctx_t[:, k, :], lambda k: w_o[:, k, :]).then_inc(wo_done, 1)

            all_slots(pe, slot)

            pe.wait_ge(slots_ready, PAIRS)
            for n in range(EXPERTS):
                g, j = divmod(n, 4)
                last = two_chunks(s_ps[32 * j:32 * j + 32, 0, g * 64:(g + 1) * 64], lambda k: w_down[:, k, n, :],
                                  lambda k: slots_t[:, k, :, n * SLOTS:(n + 1) * SLOTS])
            last.then_inc(hid_done, 1)
            pe.wait_ge(hid_ready, EXPERTS)
            ys_bank = [s_ps[:, 1, :], pt_ps[:, 0, :], pt_ps[:, 1, :], vm_ps[:, :]]
            for c in range(PAIRS // 2):
                for g in range(NG):
                    last = mm(ys_bank[c][:, 0:D],
                              hidden[:, g, 4 * c:4 * c + 4, :, :].rearrange("p b e s -> p (b e s)"),
                              w_up[:, g, :], start=g == 0, stop=g == NG - 1)
                last.then_inc(ys_done, 1)
            y_bank = [qx_ps, kl_ps, o_ps]
            for p in range(PAIRS):
                pe.wait_ge(ys_ready, p + 1)
                if p < 3:
                    pe.wait_ge(h1_ready, PAIRS)
                    pe.wait_ge(combt_ready, PAIRS)
                    pe.wait_ge(dexp_ready, PAIRS)
                else:
                    pe.wait_ge(y_ready, p - 2)
                mm(y_bank[p % 3][:, 0:D], comb_t[:, p, :], y_slots[:, p, :], start=True, stop=True).then_inc(y_done, 1)
                last = mm(s_ps[0:B, 0, 0:D], cls_comb_t[:, p, :], y_slots[:, p, :], start=p == 0, stop=p == PAIRS - 1)
            last.then_inc(yc_done, 1)

        @block.vector
        def _(dve):
            dve.memset(v_pairs[:, :, :, :], 0.0).then_inc(slot_step, 1)
            dve.memset(comb[:, :, :], 0.0).then_inc(slot_step, 1)
            dve.memset(hidden[:, :, :, :, :], 0.0).then_inc(hidden_zero, 1)
            dve.wait_ge(slot_step, 2)
            dve.memset(v_pairs[0:64, :, :, 2 * HD:2 * HD + 1], 1.0).then_inc(slot_step, 1)
            dve.memset(v_pairs[64:128, :, :, 2 * HD + 1:VW], 1.0).then_inc(slot_step, 1)

            def cls_norm():
                dve.wait_ge(in_a, 16)
                dve.bn_stats(c_bn[:, :], cls_in[0:64]).then_inc(cls_step, 1)
                dve.wait_ge(cls_step, CLS["stats"])
                dve.bn_aggr(c_mv[:, :], c_bn[:, :]).then_inc(cls_step, 1)
                dve.wait_ge(cls_step, CLS["mean"])
                dve.tensor_scalar(c_rstd[:, 0:1], c_mv[:, 1:2], LN_EPS, None, ALU.add).then_inc(cls_step, 1)
                dve.wait_ge(cls_step, CLS["rstd"])
                dve.tensor_scalar(cls_ln[:, :], cls_in[0:64], c_mv[:, 0:1], c_rstd[:, 1:2], ALU.subtract, ALU.mult)\
                   .then_inc(cls_step, 1)
                dve.wait_ge(cls_step, CLS["ln_t"])
                for k in range(KC):
                    last = dve.tensor_copy(ln1_t[:, k, :, 0], cls_ln_t[:, k, 0:2])
                last.then_inc(cls_col, 1)

            def cls_value():
                dve.wait_ge(cls_step, CLS["v_ps"])
                dve.tensor_tensor(cls_v[:, :], cls_ps[0:64, 0:D], b_v[0:64], ALU.add).then_inc(cls_step, 1)
                dve.wait_ge(cls_step, CLS["v"])
                dve.tensor_copy(cls_v_heads[:, :, 0:2 * HD], cls_v[0:HEADS].rearrange("h (p w) -> h p w", p=HP))\
                   .then_inc(cls_step, 1)
                dve.wait_ge(cls_step, CLS["v_heads"])
                dve.wait_ge(const_a, CLS_HEADS)
                dve.tensor_tensor(cls_v_heads[:, :, 0:2 * HD], cls_v_heads[:, :, 0:2 * HD],
                                  cls_head_mask[:, :, 0:2 * HD], ALU.mult)
                dve.tensor_copy(cls_v_heads[:, :, 2 * HD:VW], cls_head_mask[:, :, 2 * HD:VW])\
                   .then_inc(cls_col, 1)

            def norm2(bn, mv, s, src, dst, step, base):
                settled(dve)
                dve.bn_stats(bn[:, :], src).then_inc(step, 1)
                dve.wait_ge(step, base + 1)
                settled(dve)
                dve.bn_aggr(mv[:, :], bn[:, :]).then_inc(step, 1)
                dve.wait_ge(step, base + 2)
                dve.tensor_scalar(s[:, 0:1], mv[:, 1:2], LN_EPS, None, ALU.add)
                dve.tensor_scalar(s[:, 1:2], mv[:, 1:2], float(D), None, ALU.mult).then_inc(step, 1)
                dve.wait_ge(step, base + 4)
                dve.tensor_scalar(s[:, 4:5], s[:, 2:3], L2_EPS, s[:, 3:4], ALU.mult, ALU.add).then_inc(step, 1)
                dve.wait_ge(step, base + 5)
                dve.reciprocal(s[:, 5:6], s[:, 4:5]).then_inc(step, 1)
                dve.wait_ge(step, base + 6)
                dve.tensor_scalar(dst, src, mv[:, 0:1], s[:, 5:6], ALU.subtract, ALU.mult).then_inc(step, 1)

            def cls_output():
                dve.wait_ge(cls_step, CLS["wo_ps"])
                dve.tensor_tensor(cls_h[:, :], cls_ps[0:64, 0:D], b_o[0:64], ALU.add).then_inc(cls_col, 1)
                dve.wait_ge(cls_col, 3)
                dve.tensor_tensor(cls_h[:, :], cls_h[:, :], cls_in[0:64], ALU.add).then_inc(cls_step, 1)
                dve.wait_ge(cls_step, CLS["h"])
                norm2(c2_bn, c2_mv, c2_s, cls_h[:, :], cls_xn[:, :], cls_step, CLS["h"])

            def cls_logits():
                dve.wait_ge(cls_step, CLS["xn_t"])
                for k in range(KC):
                    last = dve.tensor_copy(xn_t[:, k, 128:129], cls_xn_t[:, k, 0:1])
                last.then_inc(cls_xn_col, 1)
                dve.wait_ge(cls_step, CLS["logits"])
                dve.tensor_reduce(cc_max[:, :], cls_ps[0:64, 0:NS], AX.X, ALU.max, negate=True).then_inc(cls_step, 1)
                dve.wait_ge(cls_step, CLS["exp"])
                dve.reciprocal(cc_inv[:, :], cc_sum[:, :]).then_inc(cls_step, 1)
                dve.wait_ge(cls_step, CLS["inv"])
                for b in range(2):
                    last = dve.tensor_scalar(cc[:, b, :], cc_exp[:, :], cc_inv[:, 0:1], None, ALU.mult)
                last.then_inc(cls_step, 1)
                dve.wait_ge(cls_step, CLS["comb_turned"])
                dve.wait_ge(const_a, CONSTANTS)
                dve.tensor_scalar(cls_comb_t[:, :, :], cls_row_mask[:, :, :], cls_ps[0:64, 0:1], None, ALU.mult)\
                   .then_inc(cls_step, 1)

            def slot_directions():
                dve.wait_ge(in_c, 16)
                dve.tensor_tensor(slot_sq[:, :, :], slots_in, slots_in, ALU.mult).then_inc(slot_step, 1)
                dve.wait_ge(slot_step, 5)
                dve.tensor_reduce(slot_ss[:, :, :], slot_sq[:, :, :].rearrange("d k (n s) -> d k s n", s=SLOTS),
                                  AX.X, ALU.add).then_inc(slot_step, 1)
                dve.wait_ge(slot_step, 7)
                dve.tensor_scalar(slot_ss[:, :, :], slot_ss[:, :, :], L2_EPS, None, ALU.add).then_inc(slot_step, 1)
                dve.wait_ge(slot_step, 8)
                dve.reciprocal(slot_inv[:, :, :], slot_ss[:, :, :]).then_inc(slot_step, 1)
                dve.wait_ge(slot_step, 9)
                dve.tensor_scalar(slot_inv[:, :, :], slot_inv[:, :, :], slot_scale[0:DC], None, ALU.mult)\
                   .then_inc(slot_inv_ready, 1)
                dve.wait_ge(slot_inv_ready, 1)
                for k in range(KC):
                    for b in range(2):
                        last = dve.tensor_tensor(
                            slot_dirs[:, k, b, :].rearrange("d (n s) -> d n s", s=SLOTS),
                            slots_in[:, k, :].rearrange("d (n s) -> d n s", s=SLOTS),
                            slot_inv[:, k, :].unsqueeze(1).to_broadcast([DC, EXPERTS, SLOTS]), ALU.mult)
                last.then_inc(slot_step, 1)

            def slot(t, there):
                early = isinstance(t, int)
                if early and t == -2:
                    cls_norm()
                if there(0):
                    p = t
                    dve.wait_ge(s_done, p + 1)
                    src = s_ps[:, :, 0:HC * TOK].rearrange("p m (h j) -> p m h j", j=TOK)
                    dve.tensor_reduce(s_max[:, :].rearrange("p (m h) -> p m h", m=KC), src, AX.X, ALU.max)\
                       .then_inc(smax_ready, 1)
                    dve.wait_ge(smax_ready, p + 1)
                    has(dve, probs_ready, p)
                    for m in range(KC):
                        last = dve.tensor_tensor(
                            s_sub[:, m * HC:(m + 1) * HC, :], src[:, m],
                            s_max[:, m * HC:(m + 1) * HC].unsqueeze(2).to_broadcast([128, HC, TOK]), ALU.subtract)
                    last.then_inc(ssub_ready, 1)
                if there(-1):
                    p = t - 1
                    dve.wait_ge(wo_done, p + 1)
                    dve.wait_ge(hbo_ready, p + 1)
                    dve.tensor_tensor(h_all[:, p, :], o_ps[:, 0:D], h_all[:, p, :], ALU.add).then_inc(h1_ready, 1)
                    dve.wait_ge(h1_ready, p + 1)
                    has(dve, xx_done, p)
                    norm2(ln2_bn, ln2_mv, ln2_s, h_all[:, p, :], xn[:, :], ln2_step, LN2_STEPS * p)
                if there(1):
                    p = t + 1
                    dve.wait_ge(k_ready, p + 1)
                    has(dve, s_done, p)
                    if early and p == 0:
                        dve.wait_ge(const_a, HEAD_MASK)
                    for h in range(ACT_HEADS, HC):
                        last = dve.tensor_scalar(k_heads[:, :, :, h, :],
                                                 k_t[:, :, :].rearrange("d m (b j) -> d m b j", j=TOK),
                                                 head_mask[:, h:h + 1], None, ALU.mult)
                    last.then_inc(km_dve_ready, 1)
                if there(-1):
                    p = t - 1
                    dve.wait_ge(ll_done, p + 1)
                    has(dve, cexp_ready, p)
                    has(dve, dexp_ready, p)
                    dve.tensor_reduce(c_max[:, :], kl_ps[:, 0:NS], AX.X, ALU.max, negate=True).then_inc(cmax_ready, 1)
                    dve.tensor_reduce(d_max[:, :], kl_ps[0:64, 64:64 + 129], AX.X, ALU.max, negate=True)\
                       .then_inc(dmax_ready, 1)
                if there(2):
                    p = t + 2
                    dve.wait_ge(tok_done, p + 1)
                    has(dve, hbo_ready, p)
                    has(dve, ln1_step, LN1_STEPS * p)
                    dve.tensor_tensor(h_tok[:, :], vm_ps[:, 0:D], b_tok, ALU.add).then_inc(h_ready, 1)
                    dve.wait_ge(h_ready, p + 1)
                    dve.bn_stats(ln1_bn[:, :], h_tok[:, :]).then_inc(ln1_step, 1)
                    dve.wait_ge(ln1_step, LN1_STEPS * p + 1)
                    settled(dve)
                    dve.bn_aggr(ln1_mv[:, :], ln1_bn[:, :]).then_inc(ln1_step, 1)
                    dve.wait_ge(ln1_step, LN1_STEPS * p + 2)
                    dve.tensor_scalar(ln1_rstd[:, 0:1], ln1_mv[:, 1:2], LN_EPS, None, ALU.add).then_inc(ln1_step, 1)
                    dve.wait_ge(ln1_step, LN1_STEPS * p + 4)
                    has(dve, ln1t_done, p)
                    dve.tensor_scalar(ln1[:, :], h_tok[:, :], ln1_mv[:, 0:1], ln1_rstd[:, 1:2],
                                      ALU.subtract, ALU.mult).then_inc(ln1_step, 1)
                if early and t == -2:
                    cls_value()
                    slot_directions()
                if early and t == -1:
                    cls_output()
                if early and t == 0:
                    cls_logits()
                if there(0):
                    p = t
                    dve.wait_ge(pv_done, p + 1)
                    o = o_ps[:, 0:HP * VW].rearrange("p (i w) -> p i w", w=VW)
                    dve.reciprocal(p_inv[:, :].rearrange("p (i e) -> p i e", e=2), o[:, :, 2 * HD:VW])\
                       .then_inc(pinv_ready, 1)
                    dve.wait_ge(pinv_ready, p + 1)
                    has(dve, ot_done, p)
                    dve.tensor_tensor(
                        ctx_n[:, :].rearrange("p (i e d) -> p i e d", e=2, d=HD),
                        o[:, :, 0:2 * HD].rearrange("p i (e d) -> p i e d", e=2),
                        p_inv[:, :].rearrange("p (i e) -> p i e", e=2).unsqueeze(3).to_broadcast([128, HP, 2, HD]),
                        ALU.mult).then_inc(ctx_ready, 1)
                if there(-1):
                    p = t - 1
                    dve.wait_ge(cexp_ready, p + 1)
                    dve.reciprocal(c_inv[:, :], c_sum[:, :]).then_inc(cinv_ready, 1)
                    dve.wait_ge(dexp_ready, p + 1)
                    dve.reciprocal(d_inv[:, :], d_sum[:, :]).then_inc(dinv_ready, 1)
                    dve.wait_ge(cinv_ready, p + 1)
                    has(dve, dc_done, p)
                    has(dve, dcls_ready, p)
                    for b in range(2):
                        last = dve.tensor_scalar(comb[64 * b:64 * b + 64, b, :], c_exp[64 * b:64 * b + 64, :],
                                                 c_inv[64 * b:64 * b + 64, 0:1], None, ALU.mult)
                    last.then_inc(comb_ready, 1)
                    dve.wait_ge(dinv_ready, p + 1)
                    dve.tensor_scalar(disp[:, :], d_exp[:, :], d_inv[:, 0:1], None, ALU.mult).then_inc(disp_ready, 1)
                if there(1):
                    p = t + 1
                    dve.wait_ge(v_done, p + 1)
                    has(dve, pv_done, p)
                    for b in range(2):
                        rows = slice(64 * b, 64 * b + 64)
                        for e in range(2):
                            head = lambda x: x[rows].rearrange("p (i e d) -> p e i d", e=2, d=HD)[:, e]
                            last = dve.tensor_tensor(v_pairs[64 * e:64 * e + 64, b, :, HD * e:HD * e + HD],
                                                     head(vm_ps[:, 0:D]), head(b_v), ALU.add)
                    last.then_inc(v_ready, 1)

            all_slots(dve, slot)

            ys_bank = [s_ps[:, 1, :], pt_ps[:, 0, :], pt_ps[:, 1, :], vm_ps[:, :]]
            y_bank = [qx_ps, kl_ps, o_ps]

            def token_output(p):
                dve.wait_ge(y_done, p + 1)
                dve.tensor_tensor(h_all[:, p, :], y_bank[p % 3][:, 0:D], h_all[:, p, :], ALU.add).then_inc(y_ready, 1)

            for c in range(PAIRS // 2):
                dve.wait_ge(ys_done, c + 1)
                for b in range(2):
                    rows = slice(64 * b, 64 * b + 64)
                    dve.tensor_tensor(y_slots[:, 2 * c + b, :], ys_bank[c][rows, 0:D], b_up[rows], ALU.add)\
                       .then_inc(ys_ready, 1)
                if c > 0:
                    token_output(2 * c - 2)
                    token_output(2 * c - 1)
            token_output(PAIRS - 2)
            token_output(PAIRS - 1)
            dve.wait_ge(yc_done, 1)
            dve.tensor_tensor(cls_out[:, :], s_ps[0:B, 0, 0:D], cls_h[0:B, :], ALU.add).then_inc(yc_ready, 1)

        @block.scalar
        def _(act):
            act.dma_start(pa[:, :], pack_a).then_inc(in_a, 16)

            def slot(t, there):
                early = isinstance(t, int)
                if early and t == -2:
                    act.wait_ge(cls_step, CLS["ln_turned"])
                    act.activation(cls_ln_t[:, :, :], cls_ps[0:DC, 0:128].rearrange("p (k r) -> p k r", k=KC),
                                   ACT.Copy).then_inc(cls_step, 1)
                if there(0):
                    p = t
                    act.wait_ge(ssub_ready, p + 1)
                    has(act, ptb_done, p)
                    act.activation(probs[:, :, :], s_sub[:, :, 1:TOK], ACT.Exp, scale=SM_SCALE)
                    act.activation(probs_cls[:, :], s_sub[:, :, 0], ACT.Exp, scale=SM_SCALE).then_inc(probs_ready, 1)
                if there(1):
                    p = t + 1
                    act.wait_ge(qk_done, p + 1)
                    has(act, s_done, p)
                    for m in range(KC):
                        last = act.activation(q_t[:, m, :], qx_ps[0:DC, m * 128:(m + 1) * 128], ACT.Identity,
                                              bias=b_q[0:DC, m:m + 1])
                    last.then_inc(q_ready, 1)
                    has(act, km_dve_ready, p)
                    for m in range(KC):
                        last = act.activation(k_t[:, m, :], kl_ps[0:DC, m * 2 * TOK:(m + 1) * 2 * TOK], ACT.Identity,
                                              bias=b_k[0:DC, m:m + 1])
                    last.then_inc(k_ready, 1)
                    if early and p == 0:
                        act.wait_ge(const_a, HEAD_MASK)
                    act.wait_ge(k_ready, p + 1)
                    for h in range(ACT_HEADS):
                        last = act.activation(k_heads[:, :, :, h, :],
                                              k_t[:, :, :].rearrange("d m (b j) -> d m b j", j=TOK), ACT.Copy,
                                              scale=head_mask[:, h:h + 1])
                    last.then_inc(km_act_ready, 1)
                if early and t == -1:
                    act.wait_ge(cls_step, CLS["v_turned"])
                    act.activation(cls_v_t[:, :, :], cls_ps[0:DC, 0:128].rearrange("p (k r) -> p k r", k=KC),
                                   ACT.Copy).then_inc(cls_step, 1)
                if early and t == 0:
                    act.wait_ge(cls_step, CLS["xn_turned"])
                    act.activation(cls_xn_t[:, :, :], cls_ps[0:DC, 0:128].rearrange("p (k r) -> p k r", k=KC),
                                   ACT.Copy).then_inc(cls_step, 1)
                    act.wait_ge(cls_step, CLS["max"])
                    act.activation(cc_exp[:, :], cls_ps[0:64, 0:NS], ACT.Exp, bias=cc_max[:, 0:1],
                                   accum_out=cc_sum[:, 0:1]).then_inc(cls_step, 1)
                if there(-1):
                    p = t - 1
                    act.wait_ge(xnt_done, p + 1)
                    has(act, ll_done, p)
                    act.activation(xn_t[:, :, 0:128], qx_ps[0:DC, 0:256].rearrange("p (k r) -> p k r", k=KC),
                                   ACT.Copy).then_inc(xnt_ready, 1)
                if there(0):
                    p = t
                    act.wait_ge(pta_done, p + 1)
                    has(act, pv_done, p)
                    act.activation(probs_t[:, 0:4, :], pt_ps[:, 0, :].rearrange("p (i q) -> p i q", i=4),
                                   ACT.Copy).then_inc(pta_ready, 1)
                    act.wait_ge(ptb_done, p + 1)
                    act.activation(probs_t[:, 4:HP, :], pt_ps[:, 1, 0:256].rearrange("p (i q) -> p i q", i=2),
                                   ACT.Copy)
                    act.activation(probs_cls_t[:, :], pt_ps[0:HEADS, 1, 256:384], ACT.Copy).then_inc(ptb_ready, 1)
                if there(-1):
                    p = t - 1
                    act.wait_ge(cmax_ready, p + 1)
                    act.wait_ge(dmax_ready, p + 1)
                    has(act, comb_ready, p)
                    act.activation(c_exp[:, :], kl_ps[:, 0:NS], ACT.Exp, bias=c_max[:, 0:1],
                                   accum_out=c_sum[:, 0:1]).then_inc(cexp_ready, 1)
                    has(act, disp_ready, p)
                    act.activation(d_exp[:, :], kl_ps[0:64, 64:64 + 129], ACT.Exp, bias=d_max[:, 0:1],
                                   accum_out=d_sum[:, 0:1]).then_inc(dexp_ready, 1)
                if there(-1):
                    p = t - 1
                    act.wait_ge(dc_done, p + 1)
                    has(act, xx_done, p)
                    act.activation(disp_t[:, :], qx_ps[:, 0:64], ACT.Copy).then_inc(dispt_ready, 1)
                    act.activation(comb_t[:, p, :], qx_ps[0:64, 128:256], ACT.Copy).then_inc(combt_ready, 1)
                if there(0):
                    p = t
                    act.wait_ge(ot_done, p + 1)
                    has(act, wo_done, p)
                    act.activation(ctx_t[:, :, :], kl_ps[0:DC, 0:256].rearrange("p (k r) -> p k r", k=KC),
                                   ACT.Copy).then_inc(ctxt_ready, 1)
                if there(2):
                    p = t + 2
                    act.wait_ge(ln1t_done, p + 1)
                    has(act, v_done, p)
                    for k in range(KC):
                        last = act.activation(ln1_t[:, k, :, 1:TOK],
                                              o_ps[0:DC, k * 128:(k + 1) * 128].rearrange("p (b r) -> p b r", b=2),
                                              ACT.Copy)
                    if early and p == 0:
                        act.wait_ge(cls_col, 1)
                    last.then_inc(ln1t_ready, 1)
                if there(-1):
                    p = t - 1
                    act.wait_ge(xx_done, p + 1)
                    act.activation(slots_t[:, :, bass.ds(2 * p, 2), :].rearrange("d k b s -> d k (b s)"),
                                   vm_ps[0:DC, 0:128].rearrange("p (k r) -> p k r", k=KC),
                                   ACT.Copy).then_inc(slots_ready, 1)

            all_slots(act, slot)

            act.wait_ge(hid_done, 1)
            act.wait_ge(hidden_zero, 1)
            for n in range(EXPERTS):
                g, j = divmod(n, 4)
                rows = slice(32 * j, 32 * j + 32)
                act.activation(hidden[rows, g, :, n, :],
                               s_ps[rows, 0, g * 64:(g + 1) * 64].rearrange("p (b s) -> p b s", s=SLOTS),
                               ACT.Gelu, bias=b_down[rows, g:g + 1]).then_inc(hid_ready, 1)
            for p in range(PAIRS):
                act.wait_ge(y_ready, p + 1)
                act.dma_start(out[2 * p + 1, 1:TOK, :], h_all[64:128, p, :]).then_inc(out_act, 16)
            act.wait_ge(out_act, 16 * PAIRS)


def _packed(np, fields, arrays, rows):
    got = np.zeros((rows, width(fields)), np.float32)
    at = 0
    for name, n in fields:
        a = arrays[name]
        got[:a.shape[0], at:at + n] = a.reshape(a.shape[0], n)
        at += n
    return got


def kernel(**inputs):
    import numpy as np
    import concourse.bacc as bacc
    from concourse.bass_utils import run_bass_kernel_spmd

    a = {k.removeprefix("L0_"): np.asarray(v) for k, v in inputs.items()}
    side = 8
    x = a["x"].reshape(PAIRS, 2, side, 16, side, 16, 3).transpose(0, 3, 5, 6, 1, 2, 4)
    x = x.reshape(PAIRS, PC, 128, 128).transpose(0, 2, 1, 3)
    wt = a["tok_W"].reshape(PC, 128, D).transpose(1, 0, 2)

    def rows(v, n=128):
        return np.broadcast_to(v.reshape(1, -1), (n, v.size))

    def chunks(w):
        return w.reshape(KC, DC, -1).transpose(1, 0, 2)

    def heads(w):
        return chunks(w.transpose(1, 0, 2).reshape(D, D))

    wdown = np.zeros((DC, KC, EXPERTS, QW), np.float32)
    wdown[:, :, :, :HID] = chunks(a["ffn_W_down"].transpose(1, 0, 2)).reshape(DC, KC, EXPERTS, HID)
    wup = np.zeros((4, QW, NG, D), np.float32)
    wup[:, :HID] = a["ffn_W_up"].reshape(NG, 4, HID, D).transpose(1, 2, 0, 3)
    bdown = np.zeros((4, QW, NG), np.float32)
    bdown[:, :HID] = a["ffn_b_down"].reshape(NG, 4, HID).transpose(1, 2, 0)
    bup = np.broadcast_to(a["ffn_b_up"][None, :, None, :], (4, EXPERTS, SLOTS, D)).reshape(128, D)
    pack_a = _packed(np, FIELDS_A, {
        "cls": rows(a["cls_tok"]), "btok": rows(a["tok_b"]), "bo": rows(a["attn_bo"]), "bv": rows(a["attn_bv"]),
        "bq": a["attn_bq"].reshape(KC, DC).T, "bk": a["attn_bk"].reshape(KC, DC).T,
        "scale": rows(a["ffn_scale"])}, 128)
    pack_b = _packed(np, FIELDS_B, {
        "wq": heads(a["attn_Wq"]), "wk": heads(a["attn_Wk"]), "wv": heads(a["attn_Wv"])}, DC)
    pack_c = _packed(np, FIELDS_C, {
        "wo": chunks(a["attn_Wo"]), "slots": chunks(a["ffn_slot_params"].reshape(D, NS)), "wdown": wdown,
        "wup": wup.reshape(128, NG * D), "bdown": bdown.reshape(128, NG), "bup": bup}, 128)

    nc = bacc.Bacc("TRN2", target_bir_lowering=False, num_devices=1)
    arrays, args = {}, []
    for name, v in (("xt", x), ("wtok", wt), ("pack_a", pack_a), ("pack_b", pack_b), ("pack_c", pack_c)):
        arrays[name] = np.ascontiguousarray(v)
        args.append(nc.dram_tensor(name, arrays[name].shape, F32, kind="ExternalInput").ap())
    args.append(nc.dram_tensor("out", (B, TOK, D), F32, kind="ExternalOutput").ap())
    vit_tower_kernel(nc, *args)
    r = run_bass_kernel_spmd(nc, [arrays], core_ids=[0])
    return r.results[0]["out"]
```

```python
from contextlib import ExitStack

import concourse.bass as bass
from concourse import mybir

F32 = mybir.dt.float32
BF16 = mybir.dt.bfloat16
ALU = mybir.AluOpType
ACT = mybir.ActivationFunctionType
AX = mybir.AxisListType

B, NPATCH, D, PIX = 16, 64, 192, 768
HEADS, HD = 12, 16
TOK = NPATCH + 1
EXPERTS, SLOTS, HID = 8, 4, 24
NS = EXPERTS * SLOTS
PAIRS = B // 2
KC = 2
DC = D // KC
PC = PIX // 128
HC = HEADS // KC
HP = HEADS // 2
HPC = HP // KC
VW = 2 * HD + 2
QW = 32
NG = EXPERTS // 4
GROUPS = B // 4
EARLY_IMAGES = B - 4
ACT_HEADS = 3
SM_SCALE = HD ** -0.5
LN_EPS = 1e-5
L2_EPS = 1e-6
MASKED = -1e30

FIELDS_A = [("cls", D), ("btok", D), ("bo", D), ("bv", D), ("bq", KC), ("bk", KC), ("scale", 1)]
FIELDS_B = [("wq", KC * D), ("wk", KC * D), ("wv", KC * D)]
FIELDS_C = [("wo", KC * D), ("slots", KC * NS), ("wdown", KC * EXPERTS * QW), ("wup", NG * D), ("bdown", NG), ("bup", D)]


def width(fields):
    return sum(n for _, n in fields)


def offsets(fields):
    at, out = 0, {}
    for name, n in fields:
        out[name] = (at, n)
        at += n
    return out


def vit_tower_kernel(nc, xt, wtok, pack_a, pack_b, pack_c, out_tok, out_cls):
    with ExitStack() as ctx:
        def sb(name, shape, dt=F32):
            return ctx.enter_context(nc.sbuf_tensor(name, shape, dt))

        def sem(name):
            return ctx.enter_context(nc.semaphore(name))

        ident = sb("ident", [128, 128])
        ident_b = sb("ident_b", [128, 128], BF16)
        causal = sb("causal", [128, HC, TOK], BF16)
        slot_mask = sb("slot_mask", [64, 129], BF16)
        head_mask = sb("head_mask", [DC, HC])
        cls_head_mask = sb("cls_head_mask", [HEADS, HP, VW])
        cls_row_mask = sb("cls_row_mask", [128, GROUPS, B])
        powers = sb("powers", [128, 3])
        halves = sb("halves", [DC, KC, SLOTS])

        wt = sb("wt", [128, PC, D])
        pa = sb("pa", [128, width(FIELDS_A)])
        pb = sb("pb", [DC, width(FIELDS_B)])
        pc = sb("pc", [128, width(FIELDS_C)])

        def field(name):
            for tile, fields in ((pa, FIELDS_A), (pb, FIELDS_B), (pc, FIELDS_C)):
                if name in offsets(fields):
                    a, n = offsets(fields)[name]
                    return tile[:, a:a + n]

        cls_in, b_tok, b_o, b_v = field("cls"), field("btok"), field("bo"), field("bv")
        b_q, b_k, slot_scale = field("bq"), field("bk"), field("scale")
        w_q = field("wq").rearrange("p (k n) -> p k n", k=KC)
        w_k = field("wk").rearrange("p (k n) -> p k n", k=KC)
        w_v = field("wv").rearrange("p (k n) -> p k n", k=KC)
        w_o = field("wo")[0:DC].rearrange("p (k n) -> p k n", k=KC)
        slots_in = field("slots")[0:DC].rearrange("p (k n) -> p k n", k=KC)
        w_down = field("wdown")[0:DC].rearrange("p (k e h) -> p k e h", k=KC, e=EXPERTS)
        w_up = field("wup").rearrange("p (g n) -> p g n", g=NG)
        b_down, b_up = field("bdown"), field("bup")

        slot_sq = sb("slot_sq", [DC, KC, NS])
        slot_ss = sb("slot_ss", [DC, KC, SLOTS])
        slot_inv = sb("slot_inv", [DC, KC, SLOTS])
        slot_dirs = sb("slot_dirs", [DC, KC, 2, NS])

        xt_first = sb("xt_first", [128, PC, 128])
        xt_next = sb("xt_next", [128, PC, 128])
        h_tok = sb("h_tok", [128, D])
        ln1_bn = sb("ln1_bn", [128, 6])
        ln1_mv = sb("ln1_mv", [128, 2])
        ln1_rstd = sb("ln1_rstd", [128, 2])
        ln1 = sb("ln1", [128, D])
        ln1_t = sb("ln1_t", [DC, KC, 2, TOK])
        q_t = sb("q_t", [DC, KC, 128])
        k_t = sb("k_t", [DC, KC, 2 * TOK])
        k_heads = sb("k_heads", [DC, KC, 2, HC, TOK])
        v_pairs = sb("v_pairs", [128, 2, HP, VW])
        s_max = sb("s_max", [128, HEADS])
        s_sub = sb("s_sub", [128, HEADS, TOK])
        probs = sb("probs", [128, HEADS, NPATCH])
        probs_cls = sb("probs_cls", [128, HEADS])
        probs_t = sb("probs_t", [128, HP, 128])
        probs_cls_t = sb("probs_cls_t", [HEADS, 128])
        p_inv = sb("p_inv", [128, HEADS])
        ctx_n = sb("ctx_n", [128, D])
        ctx_t = sb("ctx_t", [DC, KC, 128])
        ln2_bn = sb("ln2_bn", [128, 6])
        ln2_mv = sb("ln2_mv", [128, 2])
        ln2_s = sb("ln2_s", [128, 7])
        xn = sb("xn", [128, D])
        xn_t = sb("xn_t", [DC, KC, 129])
        c_max = sb("c_max", [128, 1])
        c_exp = sb("c_exp", [128, NS])
        c_sum = sb("c_sum", [128, 1])
        c_inv = sb("c_inv", [128, 1])
        comb = sb("comb", [128, 2, 2, NS])
        d_max = sb("d_max", [64, 1])
        d_exp = sb("d_exp", [64, 129])
        d_sum = sb("d_sum", [64, 1])
        d_inv = sb("d_inv", [64, 1])
        disp = sb("disp", [64, 129])
        disp_t = sb("disp_t", [128, 64])
        disp_cls = sb("disp_cls", [64, 64])

        h_all = sb("h_all", [128, PAIRS, D])
        comb_t = sb("comb_t", [128, PAIRS, 128])
        slots_t = sb("slots_t", [DC, KC, B, NS])
        hidden = sb("hidden", [128, NG, B, EXPERTS, SLOTS])
        y_slots = sb("y_slots", [128, GROUPS, D])

        c_bn = sb("c_bn", [64, 6])
        c_mv = sb("c_mv", [64, 2])
        c_rstd = sb("c_rstd", [64, 2])
        cls_ln = sb("cls_ln", [64, D])
        cls_ln_t = sb("cls_ln_t", [DC, KC, 64])
        cls_v = sb("cls_v", [64, D])
        cls_v_heads = sb("cls_v_heads", [HEADS, HP, VW])
        cls_v_t = sb("cls_v_t", [DC, KC, 64])
        cls_h = sb("cls_h", [64, D])
        c2_bn = sb("c2_bn", [64, 6])
        c2_mv = sb("c2_mv", [64, 2])
        c2_s = sb("c2_s", [64, 7])
        cls_xn = sb("cls_xn", [64, D])
        cls_xn_t = sb("cls_xn_t", [DC, KC, 64])
        cc_max = sb("cc_max", [64, 1])
        cc_exp = sb("cc_exp", [64, NS])
        cc_sum = sb("cc_sum", [64, 1])
        cc_inv = sb("cc_inv", [64, 1])
        cc = sb("cc", [64, 4, NS])
        cls_comb_t = sb("cls_comb_t", [128, GROUPS, B])
        cls_out = sb("cls_out", [B, D])
        idle = sb("idle", [128, 2 * 128], BF16)
        table = sb("table", [128, 1])

        bank = [ctx.enter_context(nc.psum_tensor(f"bank{i}", [128, 512], F32)) for i in (4, 5, 6, 7)]
        s_ps = ctx.enter_context(nc.psum_tensor("s_ps", [128, KC, 512], F32))
        pt_ps = ctx.enter_context(nc.psum_tensor("pt_ps", [128, 2, 512], F32))
        qx_ps, kl_ps, vm_ps, o_ps = bank
        cls_ps = pt_ps[:, 0, :]
        cls_end_ps = s_ps[:, 1, :]
        hid_ps = s_ps[:, 0, :]
        ys_bank = [s_ps[:, 1, :], pt_ps[:, 0, :], pt_ps[:, 1, :], vm_ps]
        y_bank = [o_ps, pt_ps[:, 0, :], pt_ps[:, 1, :]]
        yc_ps = s_ps[:, 1, :]

        in_next, in_a, in_b, in_c = (sem(n) for n in ("in_next", "in_a", "in_b", "in_c"))
        in_first, in_wt = [sem("in_first_0"), sem("in_first_1")], [sem("in_wt_0"), sem("in_wt_1")]
        const_a, hidden_zero, slot_step, cls_step = (sem(n) for n in ("const_a", "hidden_zero", "slot_step", "cls_step"))
        idle_ready, cls_values, cls_bo, cls_xn_col, slot_inv_ready = (sem(n) for n in (
            "idle_ready", "cls_values", "cls_bo", "cls_xn_col", "slot_inv_ready"))
        (tok_done, ln1t_done, qk_done, v_done, s_done, pta_done, ptb_done, pv_done, ot_done, wo_done, xnt_done,
         ll_done, dc_done, xx_done) = (sem(n) for n in (
             "tok_done", "ln1t_done", "qk_done", "v_done", "s_done", "pta_done", "ptb_done", "pv_done", "ot_done",
             "wo_done", "xnt_done", "ll_done", "dc_done", "xx_done"))
        (h_ready, hbo_ready, ln1_step, ln1t_ready, q_ready, k_ready, km_act_ready, km_dve_ready, v_ready, smax_ready, ssub_ready,
         probs_ready, pta_ready, ptb_ready, pinv_ready, ctx_ready, ctxt_ready, h1_ready, ln2_step, xnt_ready,
         cmax_ready, cexp_ready, cinv_ready, comb_ready, dmax_ready, dexp_ready, dinv_ready, disp_ready,
         dcls_ready, dispt_ready, combt_ready, slots_ready) = (sem(n) for n in (
             "h_ready", "hbo_ready", "ln1_step", "ln1t_ready", "q_ready", "k_ready", "km_act_ready", "km_dve_ready",
             "v_ready",
             "smax_ready", "ssub_ready", "probs_ready", "pta_ready", "ptb_ready", "pinv_ready", "ctx_ready",
             "ctxt_ready", "h1_ready", "ln2_step", "xnt_ready", "cmax_ready", "cexp_ready", "cinv_ready",
             "comb_ready", "dmax_ready", "dexp_ready", "dinv_ready", "disp_ready", "dcls_ready", "dispt_ready",
             "combt_ready", "slots_ready"))
        passed = sem("passed")
        hid_done, hid_ready, ys_done, ys_ready, y_done, y_ready, yc_done, yc_ready, out_sp, out_act = (sem(n) for n in (
            "hid_done", "hid_ready", "ys_done", "ys_ready", "y_done", "y_ready", "yc_done", "yc_ready",
            "out_sp", "out_act"))
        SLOT_STEPS = 10
        WAIT_INPUTS, WAIT_EMBEDDING, WAIT_NORM1, WAIT_KEYS, WAIT_NORM2, WAIT_SOFTMAX, WAIT_GELU, WAIT_BIAS = (
            12, 6, 0, 12, 13, 6, 12, 6)
        IDENT, POWERS, HEAD_MASK, CAUSAL, CLS_HEADS, SLOT_MASK, CONSTANTS = 2, 5, 8, 12, 15, 18, 23
        LN1_STEPS, LN2_STEPS = 5, 7
        names = ("stats mean var_eps rstd ln ln_turned ln_t v_ps v v_heads v_turned v_t wo_ps h".split()
                 + [f"norm2_{i}" for i in range(1, LN2_STEPS)]
                 + "xn xn_turned xn_t logits max exp inv comb comb_turned comb_t".split())
        CLS = {name: i + 1 for i, name in enumerate(names)}

        def has(eng, s, n):
            if not isinstance(n, int) or n > 0:
                eng.wait_ge(s, n)

        def settled(eng):
            eng.sem_inc(passed, 1)

        def capped(n):
            return min(n, PAIRS) if isinstance(n, int) else n

        def all_slots(eng, run):
            def peeled(first, end):
                for t in range(first, end):
                    run(t, lambda k: 0 <= t + k < PAIRS)

            peeled(-2, 2)
            with eng.Fori(2, PAIRS - 2) as t:
                run(t, lambda k: True)
            peeled(PAIRS - 2, PAIRS - 1)

        PC_PARTS = [slice(0, PC // 2), slice(PC // 2, PC)]

        block = ctx.enter_context(nc.Block())

        @block.sync
        def _(sp):
            for i, part in enumerate(PC_PARTS):
                sp.dma_start(wt[:, part, :], wtok[:, part, :]).then_inc(in_wt[i], 16)
            sp.dma_start(xt_next[:, :, :], xt[1]).then_inc(in_next, 16)
            sp.dma_start(pb[:, :], pack_b).then_inc(in_b, 16)
            sp.dma_start(pc[:, :], pack_c).then_inc(in_c, 16)
            with sp.Fori(2, PAIRS) as p:
                sp.wait_ge(tok_done, p)
                sp.dma_start(xt_next[:, :, :], xt[p]).then_inc(in_next, 16)
            for first, end in ((0, 3), (3, PAIRS - 2), (PAIRS - 1, PAIRS)):
                sp.wait_ge(y_ready, end)
                sp.dma_start(out_tok[:, first:end, :], h_all[:, first:end, :]).then_inc(out_sp, 16)
            sp.wait_ge(yc_ready, 1)
            sp.dma_start(out_cls, cls_out[:, :]).then_inc(out_sp, 16)
            sp.wait_ge(out_sp, 16 * 4)

        @block.gpsimd
        def _(pool):
            made = [0]

            def then(instruction):
                made[0] += 1
                instruction.then_inc(const_a, 1)
                pool.wait_ge(const_a, made[0])

            def keep(tile, compare, fill, base, pattern, channel):
                then(pool.affine_select(out=tile, in_=tile, compare_op=compare, fill=fill, base=base,
                                        pattern=pattern, channel_multiplier=channel))

            then(pool.memset(ident[:, :], 0.0))
            keep(ident[:, :], ALU.not_equal, 1.0, 0, [[-1, 128]], 1)
            then(pool.memset(powers[:, 0:1], -0.5))
            then(pool.memset(powers[:, 1:3], 0.5))
            then(pool.memset(halves[:, :, :], 0.5))
            then(pool.memset(head_mask[:, :], 1.0))
            keep(head_mask[:, :], ALU.is_ge, 0.0, 0, [[-HD, HC]], 1)
            keep(head_mask[:, :], ALU.is_ge, 0.0, HD - 1, [[HD, HC]], -1)
            then(pool.tensor_copy(ident_b[:, :], ident[:, :]))
            then(pool.memset(causal[:, :, :], 0.0))
            for b in range(2):
                keep(causal[64 * b:64 * b + 64], ALU.is_ge, MASKED, 1, [[0, HC], [-1, TOK]], 1)
            then(pool.memset(cls_head_mask[:, :, :], 1.0))
            keep(cls_head_mask[:, :, 0:2 * HD].rearrange("h p (e d) -> h p e d", e=2), ALU.is_equal, 0.0, 0,
                 [[-2, HP], [-1, 2], [0, HD]], 1)
            keep(cls_head_mask[:, :, 2 * HD:VW], ALU.is_equal, 0.0, 0, [[-2, HP], [-1, 2]], 1)
            then(pool.memset(slot_mask[:, :], 0.0))
            for b in range(2):
                then(pool.memset(slot_mask[NS * b:NS * b + NS, 64 * (1 - b):64 * (1 - b) + 64], MASKED))
            then(pool.memset(cls_row_mask[:, :, :], 1.0))
            for b in range(4):
                keep(cls_row_mask[NS * b:NS * b + NS], ALU.is_equal, 0.0, -b, [[-4, GROUPS], [1, B]], 0)
            assert made[0] == CONSTANTS

            def power(dst, src, exponents, step, n):
                pool.wait_ge(step, n)
                pool.tensor_tensor(dst, src, exponents, ALU.pow).then_inc(step, 1)

            def norm1(p):
                power(ln1_rstd[:, 1:2], ln1_rstd[:, 0:1], powers[:, 0:1], ln1_step, LN1_STEPS * p + 3)
                pool.wait_ge(h_ready, p + 1)
                pool.tensor_tensor(h_all[:, p, :], h_tok[:, :], b_o, ALU.add).then_inc(hbo_ready, 1)

            def slot(t, there):
                early = isinstance(t, int)
                if early and t == -2:
                    pool.wait_ge(in_a, 16)
                    power(c_rstd[:, 1:2], c_rstd[:, 0:1], powers[0:64, 0:1], cls_step, CLS["var_eps"])
                if early and t == 0:
                    power(c2_s[:, 2:4], c2_s[:, 0:2], powers[0:64, 1:3], cls_step, CLS["norm2_3"])
                if there(-1):
                    power(ln2_s[:, 2:4], ln2_s[:, 0:2], powers[:, 1:3], ln2_step, LN2_STEPS * (t - 1) + 3)
                if there(2) and not (early and t == -1):
                    norm1(t + 2)
                if early and t == -2:
                    norm1(1)
                if early and t == -1:
                    power(slot_ss[:, :, :], slot_ss[:, :, :], halves[:, :, :], slot_step, 6)
                if there(-1):
                    p = t - 1
                    pool.wait_ge(disp_ready, p + 1)
                    has(pool, xx_done, p)
                    settled(pool)
                    pool.tensor_scalar(disp_cls[:, :], ident[0:64, 0:64], disp[:, 128:129], None,
                                       ALU.mult).then_inc(dcls_ready, 1)

            all_slots(pool, slot)
            slot(PAIRS - 1, lambda k: k <= 0)
            slot(PAIRS, lambda k: k < 0)

        @block.tensor
        def _(pe):
            mm, tr = pe.matmul, pe.transpose

            def two_transposes(dst, src, rows):
                for kc in range(KC):
                    last = tr(dst[0:DC, kc * rows:(kc + 1) * rows], src[0:rows, kc * DC:(kc + 1) * DC],
                              ident[0:rows, 0:rows])
                return last

            def two_chunks(dst, lhs, rhs, first=True):
                for kc in range(KC):
                    last = mm(dst, lhs(kc), rhs(kc), start=first and kc == 0, stop=kc == KC - 1)
                return last

            def keep_clock(n, bank):
                for _ in range(n):
                    mm(bank[:, 0:2 * 128], idle[:, 0:128], idle[:, :], start=True, stop=True)

            def cls_part(result):
                if result == "ln_turned":
                    pe.wait_ge(cls_step, CLS["ln"])
                    two_transposes(cls_ps, cls_ln, 64).then_inc(cls_step, 1)
                if result == "v_ps":
                    pe.wait_ge(in_b, 16)
                    pe.wait_ge(cls_step, CLS["ln_t"])
                    two_chunks(cls_ps[0:64, 0:D], lambda k: cls_ln_t[:, k, :], lambda k: w_v[:, k, :])\
                        .then_inc(cls_step, 1)
                if result == "v_turned":
                    pe.wait_ge(cls_step, CLS["v_heads"])
                    two_transposes(cls_ps, cls_v, 64).then_inc(cls_step, 1)
                if result == "wo_ps":
                    pe.wait_ge(in_c, 16)
                    pe.wait_ge(cls_step, CLS["v_t"])
                    two_chunks(cls_ps[0:64, 0:D], lambda k: cls_v_t[:, k, :], lambda k: w_o[:, k, :])\
                        .then_inc(cls_step, 1)
                if result == "xn_turned":
                    pe.wait_ge(cls_step, CLS["xn"])
                    pe.wait_ge(q_ready, 2)
                    two_transposes(qx_ps, cls_xn, 64).then_inc(cls_step, 1)
                if result == "logits":
                    two_chunks(cls_end_ps[0:64, 0:NS], lambda k: cls_xn_t[:, k, :], lambda k: slot_dirs[:, k, 0, :])\
                        .then_inc(cls_step, 1)
                if result == "comb_turned":
                    pe.wait_ge(cls_step, CLS["comb"])
                    tr(cls_end_ps[:, 0:64], cc[:, :, :].rearrange("p b s -> p (b s)"), ident[0:64, 0:64])\
                        .then_inc(cls_step, 1)

            def queries_and_keys(p):
                pe.wait_ge(ln1t_ready, p + 1)
                has(pe, combt_ready, p - 2)
                has(pe, dispt_ready, p - 2)
                has(pe, ctxt_ready, p - 1)
                for m in range(KC):
                    q_rhs = lambda k: ln1_t[:, k, :, 1:TOK]
                    k_rhs = lambda k: ln1_t[:, k, :, :]
                    two_chunks(qx_ps[0:DC, m * 128:(m + 1) * 128], lambda k: w_q[:, k, m * DC:(m + 1) * DC], q_rhs)
                    last = two_chunks(kl_ps[0:DC, m * 2 * TOK:(m + 1) * 2 * TOK],
                                      lambda k: w_k[:, k, m * DC:(m + 1) * DC], k_rhs)
                last.then_inc(qk_done, 1)

            def embedding(p, first=False):
                if not first:
                    pe.wait_ge(in_next, 16 * p)
                has(pe, slots_ready, p - 3)
                if isinstance(p, int):
                    has(pe, h_ready, p)
                has(pe, v_ready, p - 1)
                x = xt_first if first else xt_next
                for c in range(PC):
                    for i, part in enumerate(PC_PARTS):
                        if first and c == part.start:
                            pe.wait_ge(in_wt[i], 16)
                            pe.wait_ge(in_first[i], 16)
                    last = mm(vm_ps[:, 0:D], x[:, c, :], wt[:, c, :], start=c == 0, stop=c == PC - 1)
                last.then_inc(tok_done, 1)

            def values(p):
                has(pe, h_ready, capped(p + 2))
                two_chunks(vm_ps[0:64, 0:D], lambda k: ln1_t[:, k, 0, 1:TOK], lambda k: w_v[:, k, :])
                two_chunks(vm_ps[64:128, 0:D], lambda k: ln1_t[:, k, 1, 1:TOK], lambda k: w_v[:, k, :])\
                    .then_inc(v_done, 1)

            def scores(p, m, early):
                if m == 0:
                    if early and p == 0:
                        pe.wait_ge(const_a, CAUSAL)
                    pe.wait_ge(q_ready, p + 1)
                    pe.wait_ge(km_act_ready, p + 1)
                    pe.wait_ge(km_dve_ready, p + 1)
                has(pe, ssub_ready, KC * (p - 1) + m + 1)
                dst = s_ps[:, m, 0:HC * TOK]
                mm(dst, ident_b[:, :], causal[:, :, :].rearrange("p h j -> p (h j)"), start=True, stop=False,
                   skip_group_check=True)
                for b in range(2):
                    last = mm(s_ps[64 * b:64 * b + 64, m, 0:HC * TOK], q_t[:, m, 64 * b:64 * b + 64],
                              k_heads[:, m, b, :, :].rearrange("d h j -> d (h j)"), start=False, stop=True,
                              skip_group_check=True)
                last.then_inc(s_done, 1)

            def turn_probs(p):
                for m, (turned, copied) in enumerate(((pta_done, pta_ready), (ptb_done, ptb_ready))):
                    pe.wait_ge(probs_ready, KC * p + m + 1)
                    has(pe, copied, p)
                    for i in range(HPC):
                        h = m * HC + 2 * i
                        last = tr(pt_ps[:, m, i * 128:(i + 1) * 128],
                                  probs[:, h:h + 2, :].rearrange("p h j -> p (h j)"), ident[:, :])
                    if m == KC - 1:
                        last = tr(pt_ps[0:HEADS, m, HPC * 128:(HPC + 1) * 128], probs_cls[:, :], ident[:, :])
                    last.then_inc(turned, 1)

            def context(p, early):
                has(pe, h1_ready, p)
                pe.wait_ge(pta_ready, p + 1)
                pe.wait_ge(ptb_ready, p + 1)
                pe.wait_ge(v_ready, p + 1)
                if early and p == 0:
                    pe.wait_ge(cls_values, 1)
                mm(o_ps[:, 0:HP * VW], probs_cls_t[:, :], cls_v_heads[:, :, :].rearrange("h p w -> h (p w)"),
                   start=True, stop=False, skip_group_check=True)
                for i in range(HP):
                    for b in range(2):
                        last = mm(o_ps[64 * b:64 * b + 64, i * VW:(i + 1) * VW],
                                  probs_t[:, i, 64 * b:64 * b + 64], v_pairs[:, b, i, :],
                                  start=False, stop=True, skip_group_check=True)
                last.then_inc(pv_done, 1)

            def turn_context(p, bank):
                pe.wait_ge(ctx_ready, p + 1)
                if bank is kl_ps:
                    has(pe, cexp_ready, p)
                    has(pe, dexp_ready, p)
                two_transposes(bank, ctx_n, 128).then_inc(ot_done, 1)

            def turn_norm1(p):
                pe.wait_ge(ln1_step, LN1_STEPS * (p + 1))
                has(pe, ctx_ready, p - 1)
                two_transposes(o_ps, ln1, 128).then_inc(ln1t_done, 1)

            def projection(p):
                pe.wait_ge(ctxt_ready, p + 1)
                has(pe, ln1t_ready, capped(p + 3))
                two_chunks(o_ps[:, 0:D], lambda k: ctx_t[:, k, :], lambda k: w_o[:, k, :]).then_inc(wo_done, 1)

            def turn_norm2(p):
                pe.wait_ge(ln2_step, LN2_STEPS * (p + 1))
                has(pe, q_ready, capped(p + 3))
                two_transposes(qx_ps, xn, 128).then_inc(xnt_done, 1)

            def logits(p, early):
                pe.wait_ge(xnt_ready, p + 1)
                has(pe, k_ready, capped(p + 3))
                if early and p == 0:
                    pe.wait_ge(cls_xn_col, 1)
                    pe.wait_ge(const_a, SLOT_MASK)
                    pe.wait_ge(slot_step, SLOT_STEPS)
                two_chunks(kl_ps[:, 0:NS], lambda k: xn_t[:, k, 0:128], lambda k: slot_dirs[:, k, 0, :])
                mm(kl_ps[0:64, 64:64 + 129], ident_b[0:64, 0:64], slot_mask[:, :], start=True, stop=False)
                two_chunks(kl_ps[0:64, 64:64 + 129],
                           lambda k: slot_dirs[:, k, :, :].rearrange("p b s -> p (b s)"),
                           lambda k: xn_t[:, k, :], first=False).then_inc(ll_done, 1)

            def turn_weights(p):
                pe.wait_ge(disp_ready, p + 1)
                pe.wait_ge(comb_ready, p + 1)
                settled(pe)
                tr(qx_ps[:, 128:256], comb[:, :, :, :].rearrange("p c b s -> p (c b s)"), ident[:, :])
                tr(qx_ps[:, 0:64], disp[:, 0:128], ident[0:64, 0:64]).then_inc(dc_done, 1)

            def slot_inputs(p):
                pe.wait_ge(dispt_ready, p + 1)
                pe.wait_ge(dcls_ready, p + 1)
                has(pe, v_ready, capped(p + 3))
                for kc in range(KC):
                    mm(vm_ps[0:DC, kc * 64:(kc + 1) * 64], xn[:, kc * DC:(kc + 1) * DC], disp_t[:, :],
                       start=True, stop=False)
                    last = mm(vm_ps[0:DC, kc * 64:(kc + 1) * 64], cls_xn[:, kc * DC:(kc + 1) * DC],
                              disp_cls[:, :], start=False, stop=True)
                last.then_inc(xx_done, 1)

            def slot(t, there):
                early = isinstance(t, int)
                if early and t == 1:
                    pe.wait_ge(cls_xn_col, 1)
                if there(1):
                    queries_and_keys(t + 1)
                if early and t == -2:
                    pe.wait_ge(idle_ready, 1)
                    keep_clock(WAIT_INPUTS, vm_ps)
                if early and t == 0:
                    pe.wait_ge(cls_bo, 1)
                    turn_probs(0)
                if there(2) and not (early and t == -1):
                    embedding(t + 2, early and t == -2)
                if early and t == -2:
                    pe.wait_ge(const_a, IDENT)
                    cls_part("ln_turned")
                    keep_clock(WAIT_EMBEDDING, o_ps)
                    embedding(1)
                    cls_part("v_ps")
                    keep_clock(WAIT_NORM1, o_ps)
                if early and t == -1:
                    values(0)
                    cls_part("v_turned")
                    keep_clock(WAIT_KEYS, o_ps)
                    cls_part("wo_ps")
                if early and t == PAIRS - 2:
                    pe.wait_ge(slots_ready, PAIRS - 3)
                    pe.wait_ge(v_ready, PAIRS - 1)
                    keep_clock(WAIT_NORM2, vm_ps)
                if there(-1):
                    turn_norm2(t - 1)
                if there(0):
                    if not (early and t == 0):
                        turn_probs(t)
                if there(-1):
                    logits(t - 1, early)
                if there(0):
                    context(t, early)
                if there(1):
                    if not (early and t == -1):
                        values(t + 1)
                    scores(t + 1, 0, early)
                if early and t == 0:
                    cls_part("xn_turned")
                if there(-1):
                    turn_weights(t - 1)
                if there(0):
                    turn_context(t, kl_ps)
                if there(1):
                    scores(t + 1, 1, early)
                if there(2):
                    turn_norm1(t + 2)
                if there(-1):
                    slot_inputs(t - 1)
                if there(0):
                    projection(t)

            def hidden_units(images):
                for n in range(EXPERTS):
                    g, j = divmod(n, 4)
                    at = g * 64 + images.start * SLOTS
                    last = two_chunks(hid_ps[32 * j:32 * j + 32, at:at + len(images) * SLOTS],
                                      lambda k: w_down[:, k, n, :],
                                      lambda k: slots_t[:, k, images.start:images.stop, n * SLOTS:(n + 1) * SLOTS])
                last.then_inc(hid_done, 1)

            def slot_outputs(c):
                for g in range(NG):
                    if c == GROUPS - 1:
                        pe.wait_ge(hid_ready, EXPERTS + 4 * (g + 1))
                    last = mm(ys_bank[c][:, 0:D],
                              hidden[:, g, 4 * c:4 * c + 4, :, :].rearrange("p b e s -> p (b e s)"),
                              w_up[:, g, :], start=g == 0, stop=g == NG - 1)
                last.then_inc(ys_done, 1)

            def token_outputs(p):
                pe.wait_ge(combt_ready, p + 1)
                if p == 0:
                    pe.wait_ge(h1_ready, PAIRS)
                pe.wait_ge(ys_ready, max(p // 2 + 1, min(p + 1, len(y_bank))))
                has(pe, y_ready, p + 1 - len(y_bank))
                half = slice(64 * (p % 2), 64 * (p % 2) + 64)
                mm(y_bank[p % 3][:, 0:D], comb_t[half, p, :], y_slots[half, p // 2, :], start=True, stop=True)\
                    .then_inc(y_done, 1)

            def cls_outputs(c):
                pe.wait_ge(ys_ready, c + 1)
                last = mm(yc_ps[0:B, 0:D], cls_comb_t[:, c, :], y_slots[:, c, :], start=c == 0, stop=c == GROUPS - 1)
                if c == GROUPS - 1:
                    last.then_inc(yc_done, 1)

            all_slots(pe, slot)

            pe.wait_ge(ssub_ready, KC * PAIRS)
            pe.wait_ge(slots_ready, EARLY_IMAGES // 2)
            hidden_units(range(0, EARLY_IMAGES))
            cls_part("logits")
            turn_probs(PAIRS - 1)
            turn_norm2(PAIRS - 2)
            pe.wait_ge(v_ready, PAIRS)
            keep_clock(WAIT_SOFTMAX, vm_ps)
            context(PAIRS - 1, True)
            logits(PAIRS - 2, True)
            pe.wait_ge(xnt_ready, PAIRS - 1)
            turn_context(PAIRS - 1, qx_ps)
            keep_clock(WAIT_SOFTMAX // 2, vm_ps)
            projection(PAIRS - 1)
            turn_weights(PAIRS - 2)
            cls_part("comb_turned")
            slot_inputs(PAIRS - 2)

            pe.wait_ge(hid_ready, EXPERTS)
            pe.wait_ge(cls_step, CLS["comb_t"])
            for c in range(GROUPS - 1):
                slot_outputs(c)
            pe.wait_ge(combt_ready, PAIRS - 1)
            turn_norm2(PAIRS - 1)
            for p in range(2):
                token_outputs(p)
            logits(PAIRS - 1, True)
            for p in range(2, EARLY_IMAGES // 2):
                token_outputs(p)
            turn_weights(PAIRS - 1)
            for c in range(GROUPS - 1):
                cls_outputs(c)
            slot_inputs(PAIRS - 1)
            keep_clock(WAIT_BIAS, o_ps)

            pe.wait_ge(slots_ready, PAIRS)
            hidden_units(range(EARLY_IMAGES, B))
            keep_clock(WAIT_GELU, qx_ps)
            slot_outputs(GROUPS - 1)
            keep_clock(WAIT_BIAS, qx_ps)
            token_outputs(PAIRS - 2)
            token_outputs(PAIRS - 1)
            cls_outputs(GROUPS - 1)

        @block.vector
        def _(dve):
            dve.memset(table[:, :], 0.0)
            dve.memset(idle[:, :], 0.0).then_inc(idle_ready, 1)
            dve.memset(v_pairs[:, :, :, :], 0.0).then_inc(slot_step, 1)
            dve.memset(comb[:, :, :, :], 0.0).then_inc(slot_step, 1)
            dve.memset(hidden[:, :, :, :, :], 0.0).then_inc(hidden_zero, 1)
            dve.wait_ge(slot_step, 2)
            dve.memset(v_pairs[0:64, :, :, 2 * HD:2 * HD + 1], 1.0).then_inc(slot_step, 1)
            dve.memset(v_pairs[64:128, :, :, 2 * HD + 1:VW], 1.0).then_inc(slot_step, 1)

            def cls_norm():
                dve.wait_ge(in_a, 16)
                dve.bn_stats(c_bn[:, :], cls_in[0:64]).then_inc(cls_step, 1)
                dve.wait_ge(cls_step, CLS["stats"])
                dve.bn_aggr(c_mv[:, :], c_bn[:, :]).then_inc(cls_step, 1)
                dve.wait_ge(cls_step, CLS["mean"])
                dve.tensor_scalar(c_rstd[:, 0:1], c_mv[:, 1:2], LN_EPS, None, ALU.add).then_inc(cls_step, 1)
                dve.wait_ge(cls_step, CLS["rstd"])
                dve.tensor_scalar(cls_ln[:, :], cls_in[0:64], c_mv[:, 0:1], c_rstd[:, 1:2], ALU.subtract, ALU.mult)\
                   .then_inc(cls_step, 1)

            def cls_value():
                dve.wait_ge(cls_step, CLS["v_ps"])
                dve.tensor_tensor(cls_v[:, :], cls_ps[0:64, 0:D], b_v[0:64], ALU.add).then_inc(cls_step, 1)
                dve.wait_ge(cls_step, CLS["v"])
                dve.tensor_copy(cls_v_heads[:, :, 0:2 * HD], cls_v[0:HEADS].rearrange("h (p w) -> h p w", p=HP))\
                   .then_inc(cls_step, 1)
                dve.wait_ge(cls_step, CLS["v_heads"])
                dve.wait_ge(const_a, CLS_HEADS)
                dve.tensor_tensor(cls_v_heads[:, :, 0:2 * HD], cls_v_heads[:, :, 0:2 * HD],
                                  cls_head_mask[:, :, 0:2 * HD], ALU.mult)
                dve.tensor_copy(cls_v_heads[:, :, 2 * HD:VW], cls_head_mask[:, :, 2 * HD:VW])\
                   .then_inc(cls_values, 1)

            def norm2_variance(bn, mv, s, src, step, base):
                settled(dve)
                dve.bn_stats(bn[:, :], src).then_inc(step, 1)
                dve.wait_ge(step, base + 1)
                settled(dve)
                dve.bn_aggr(mv[:, :], bn[:, :]).then_inc(step, 1)
                dve.wait_ge(step, base + 2)
                dve.tensor_scalar(s[:, 0:1], mv[:, 1:2], LN_EPS, None, ALU.add)
                dve.tensor_scalar(s[:, 1:2], mv[:, 1:2], float(D), None, ALU.mult).then_inc(step, 1)

            def norm2_scaled(mv, s, src, dst, step, base):
                dve.wait_ge(step, base + 4)
                dve.tensor_scalar(s[:, 4:5], s[:, 2:3], L2_EPS, s[:, 3:4], ALU.mult, ALU.add).then_inc(step, 1)
                dve.wait_ge(step, base + 5)
                dve.reciprocal(s[:, 5:6], s[:, 4:5]).then_inc(step, 1)
                dve.wait_ge(step, base + 6)
                dve.tensor_scalar(dst, src, mv[:, 0:1], s[:, 5:6], ALU.subtract, ALU.mult).then_inc(step, 1)

            def cls_output():
                dve.wait_ge(cls_step, CLS["wo_ps"])
                dve.tensor_tensor(cls_h[:, :], cls_ps[0:64, 0:D], b_o[0:64], ALU.add).then_inc(cls_bo, 1)
                dve.wait_ge(cls_bo, 1)
                dve.tensor_tensor(cls_h[:, :], cls_h[:, :], cls_in[0:64], ALU.add).then_inc(cls_step, 1)
                dve.wait_ge(cls_step, CLS["h"])
                norm2_variance(c2_bn, c2_mv, c2_s, cls_h[:, :], cls_step, CLS["h"])

            def cls_norm2():
                norm2_scaled(c2_mv, c2_s, cls_h[:, :], cls_xn[:, :], cls_step, CLS["h"])

            def cls_largest_logit():
                dve.wait_ge(cls_step, CLS["logits"])
                dve.tensor_reduce(cc_max[:, :], cls_end_ps[0:64, 0:NS], AX.X, ALU.max, negate=True)\
                   .then_inc(cls_step, 1)

            def cls_weights():
                dve.wait_ge(cls_step, CLS["exp"])
                dve.reciprocal(cc_inv[:, :], cc_sum[:, :]).then_inc(cls_step, 1)
                dve.wait_ge(cls_step, CLS["inv"])
                for b in range(4):
                    last = dve.tensor_scalar(cc[:, b, :], cc_exp[:, :], cc_inv[:, 0:1], None, ALU.mult)
                last.then_inc(cls_step, 1)

            def cls_rows():
                dve.wait_ge(cls_step, CLS["comb_turned"])
                dve.wait_ge(const_a, CONSTANTS)
                dve.tensor_scalar(cls_comb_t[:, :, :], cls_row_mask[:, :, :], cls_end_ps[:, 0:1], None, ALU.mult)\
                   .then_inc(cls_step, 1)

            def slot_directions():
                dve.wait_ge(in_c, 16)
                dve.tensor_tensor(slot_sq[:, :, :], slots_in, slots_in, ALU.mult).then_inc(slot_step, 1)
                dve.wait_ge(slot_step, 5)
                dve.tensor_reduce(slot_ss[:, :, :], slot_sq[:, :, :].rearrange("d k (n s) -> d k s n", s=SLOTS),
                                  AX.X, ALU.add).then_inc(slot_step, 1)
                dve.wait_ge(slot_step, 7)
                dve.tensor_scalar(slot_ss[:, :, :], slot_ss[:, :, :], L2_EPS, None, ALU.add).then_inc(slot_step, 1)
                dve.wait_ge(slot_step, 8)
                dve.reciprocal(slot_inv[:, :, :], slot_ss[:, :, :]).then_inc(slot_step, 1)
                dve.wait_ge(slot_step, 9)
                dve.tensor_scalar(slot_inv[:, :, :], slot_inv[:, :, :], slot_scale[0:DC], None, ALU.mult)\
                   .then_inc(slot_inv_ready, 1)
                dve.wait_ge(slot_inv_ready, 1)
                for k in range(KC):
                    for b in range(2):
                        last = dve.tensor_tensor(
                            slot_dirs[:, k, b, :].rearrange("d (n s) -> d n s", s=SLOTS),
                            slots_in[:, k, :].rearrange("d (n s) -> d n s", s=SLOTS),
                            slot_inv[:, k, :].unsqueeze(1).to_broadcast([DC, EXPERTS, SLOTS]), ALU.mult)
                last.then_inc(slot_step, 1)

            def largest_scores(p):
                src = s_ps[:, :, 0:HC * TOK].rearrange("p m (h j) -> p m h j", j=TOK)
                for m in range(KC):
                    dve.wait_ge(s_done, KC * p + m + 1)
                    dve.tensor_reduce(s_max[:, m * HC:(m + 1) * HC], src[:, m], AX.X, ALU.max).then_inc(smax_ready, 1)
                for m in range(KC):
                    dve.wait_ge(smax_ready, KC * p + m + 1)
                    has(dve, probs_ready, KC * (p - 1) + m + 1)
                    dve.tensor_tensor(
                        s_sub[:, m * HC:(m + 1) * HC, :], src[:, m],
                        s_max[:, m * HC:(m + 1) * HC].unsqueeze(2).to_broadcast([128, HC, TOK]), ALU.subtract)\
                       .then_inc(ssub_ready, 1)

            def residual_and_norm2(p):
                dve.wait_ge(wo_done, p + 1)
                dve.wait_ge(hbo_ready, p + 1)
                dve.tensor_tensor(h_all[:, p, :], o_ps[:, 0:D], h_all[:, p, :], ALU.add).then_inc(h1_ready, 1)
                dve.wait_ge(h1_ready, p + 1)
                norm2_variance(ln2_bn, ln2_mv, ln2_s, h_all[:, p, :], ln2_step, LN2_STEPS * p)
                has(dve, xx_done, p)
                norm2_scaled(ln2_mv, ln2_s, h_all[:, p, :], xn[:, :], ln2_step, LN2_STEPS * p)

            def spread_keys(p, early):
                dve.wait_ge(k_ready, p + 1)
                has(dve, s_done, KC * p)
                if early and p == 0:
                    dve.wait_ge(const_a, HEAD_MASK)
                for h in range(ACT_HEADS, HC):
                    last = dve.tensor_scalar(k_heads[:, :, :, h, :],
                                             k_t[:, :, :].rearrange("d m (b j) -> d m b j", j=TOK),
                                             head_mask[:, h:h + 1], None, ALU.mult)
                last.then_inc(km_dve_ready, 1)

            def norm1_statistics(p):
                dve.wait_ge(tok_done, p + 1)
                has(dve, hbo_ready, p)
                has(dve, ln1_step, LN1_STEPS * p)
                dve.tensor_tensor(h_tok[:, :], vm_ps[:, 0:D], b_tok, ALU.add).then_inc(h_ready, 1)
                dve.wait_ge(h_ready, p + 1)
                dve.bn_stats(ln1_bn[:, :], h_tok[:, :]).then_inc(ln1_step, 1)
                dve.wait_ge(ln1_step, LN1_STEPS * p + 1)
                settled(dve)
                dve.bn_aggr(ln1_mv[:, :], ln1_bn[:, :]).then_inc(ln1_step, 1)
                dve.wait_ge(ln1_step, LN1_STEPS * p + 2)
                dve.tensor_scalar(ln1_rstd[:, 0:1], ln1_mv[:, 1:2], LN_EPS, None, ALU.add).then_inc(ln1_step, 1)

            def norm1(p):
                dve.wait_ge(ln1_step, LN1_STEPS * p + 4)
                has(dve, ln1t_done, p)
                dve.tensor_scalar(ln1[:, :], h_tok[:, :], ln1_mv[:, 0:1], ln1_rstd[:, 1:2],
                                  ALU.subtract, ALU.mult).then_inc(ln1_step, 1)

            def largest_logits(p):
                dve.wait_ge(ll_done, p + 1)
                has(dve, cexp_ready, p)
                has(dve, dexp_ready, p)
                dve.tensor_reduce(c_max[:, :], kl_ps[:, 0:NS], AX.X, ALU.max, negate=True).then_inc(cmax_ready, 1)
                dve.tensor_reduce(d_max[:, :], kl_ps[0:64, 64:64 + 129], AX.X, ALU.max, negate=True)\
                   .then_inc(dmax_ready, 1)

            def normalise_context(p):
                dve.wait_ge(pv_done, p + 1)
                o = o_ps[:, 0:HP * VW].rearrange("p (i w) -> p i w", w=VW)
                dve.reciprocal(p_inv[:, :].rearrange("p (i e) -> p i e", e=2), o[:, :, 2 * HD:VW])\
                   .then_inc(pinv_ready, 1)
                dve.wait_ge(pinv_ready, p + 1)
                has(dve, ot_done, p)
                dve.tensor_tensor(
                    ctx_n[:, :].rearrange("p (i e d) -> p i e d", e=2, d=HD),
                    o[:, :, 0:2 * HD].rearrange("p i (e d) -> p i e d", e=2),
                    p_inv[:, :].rearrange("p (i e) -> p i e", e=2).unsqueeze(3).to_broadcast([128, HP, 2, HD]),
                    ALU.mult).then_inc(ctx_ready, 1)

            def routing_weights(p):
                dve.wait_ge(cexp_ready, p + 1)
                dve.reciprocal(c_inv[:, :], c_sum[:, :]).then_inc(cinv_ready, 1)
                dve.wait_ge(dexp_ready, p + 1)
                dve.reciprocal(d_inv[:, :], d_sum[:, :]).then_inc(dinv_ready, 1)
                dve.wait_ge(cinv_ready, p + 1)
                has(dve, dc_done, p)
                has(dve, dcls_ready, p)
                for b in range(2):
                    rows = slice(64 * b, 64 * b + 64)
                    last = dve.tensor_scalar(comb[rows, :, b, :], c_exp[rows].unsqueeze(1).to_broadcast([64, 2, NS]),
                                             c_inv[rows, 0:1], None, ALU.mult)
                last.then_inc(comb_ready, 1)
                dve.wait_ge(dinv_ready, p + 1)
                dve.tensor_scalar(disp[:, :], d_exp[:, :], d_inv[:, 0:1], None, ALU.mult).then_inc(disp_ready, 1)

            def spread_values(p):
                dve.wait_ge(v_done, p + 1)
                has(dve, pv_done, p)
                for b in range(2):
                    rows = slice(64 * b, 64 * b + 64)
                    for e in range(2):
                        head = lambda x: x[rows].rearrange("p (i e d) -> p e i d", e=2, d=HD)[:, e]
                        last = dve.tensor_tensor(v_pairs[64 * e:64 * e + 64, b, :, HD * e:HD * e + HD],
                                                 head(vm_ps[:, 0:D]), head(b_v), ALU.add)
                last.then_inc(v_ready, 1)

            def slot(t, there):
                early = isinstance(t, int)
                if early and t == -2:
                    cls_norm()
                if there(0):
                    largest_scores(t)
                if there(-1):
                    residual_and_norm2(t - 1)
                if early and t == 0:
                    cls_output()
                if there(1):
                    spread_keys(t + 1, early)
                if there(2) and not (early and t == -1):
                    norm1_statistics(t + 2)
                if early and t == 0:
                    cls_norm2()
                if there(-1):
                    largest_logits(t - 1)
                if there(2):
                    norm1(t + 2)
                if early and t == -2:
                    norm1_statistics(1)
                    cls_value()
                if there(-1):
                    routing_weights(t - 1)
                if there(0):
                    normalise_context(t)
                if there(1):
                    spread_values(t + 1)
                if early and t == -1:
                    slot_directions()

            def slot_biases(c):
                dve.wait_ge(ys_done, c + 1)
                dve.tensor_tensor(y_slots[:, c, :], ys_bank[c][:, 0:D], b_up, ALU.add).then_inc(ys_ready, 1)

            def token_residual(p):
                dve.wait_ge(y_done, p + 1)
                dve.tensor_tensor(h_all[:, p, :], y_bank[p % 3][:, 0:D], h_all[:, p, :], ALU.add).then_inc(y_ready, 1)

            all_slots(dve, slot)

            largest_scores(PAIRS - 1)
            residual_and_norm2(PAIRS - 2)
            cls_largest_logit()
            normalise_context(PAIRS - 1)
            largest_logits(PAIRS - 2)
            cls_weights()
            routing_weights(PAIRS - 2)
            cls_rows()

            residual_and_norm2(PAIRS - 1)
            for c in range(GROUPS - 1):
                slot_biases(c)
            for p in range(2):
                token_residual(p)
            largest_logits(PAIRS - 1)
            for p in range(2, 4):
                token_residual(p)
            routing_weights(PAIRS - 1)
            for p in range(4, EARLY_IMAGES // 2):
                token_residual(p)

            slot_biases(GROUPS - 1)
            for p in range(EARLY_IMAGES // 2, PAIRS):
                token_residual(p)
            dve.wait_ge(yc_done, 1)
            dve.tensor_tensor(cls_out[:, :], yc_ps[0:B, 0:D], cls_h[0:B, :], ALU.add).then_inc(yc_ready, 1)

        @block.scalar
        def _(act):
            for i, part in enumerate(PC_PARTS):
                act.dma_start(xt_first[:, part, :], xt[0, :, part, :]).then_inc(in_first[i], 16)
            act.dma_start(pa[:, :], pack_a).then_inc(in_a, 16)

            def load_table(function):
                act.wait_ge(idle_ready, 1)
                act.activation(table[:, :], table[:, :], function)

            def halves_of(ps, n):
                return ps[0:DC, 0:2 * n].rearrange("p (k r) -> p k r", k=KC)

            def exponentials(p):
                has(act, ptb_done, p)
                for m in range(KC):
                    heads = slice(m * HC, (m + 1) * HC)
                    act.wait_ge(ssub_ready, KC * p + m + 1)
                    last = act.activation(probs[:, heads, :], s_sub[:, heads, 1:TOK], ACT.Exp, scale=SM_SCALE)
                    if m == KC - 1:
                        last = act.activation(probs_cls[:, :], s_sub[:, :, 0], ACT.Exp, scale=SM_SCALE)
                    last.then_inc(probs_ready, 1)

            def queries(p):
                act.wait_ge(qk_done, p + 1)
                has(act, s_done, KC * p)
                for m in range(KC):
                    last = act.activation(q_t[:, m, :], qx_ps[0:DC, m * 128:(m + 1) * 128], ACT.Identity,
                                          bias=b_q[0:DC, m:m + 1])
                last.then_inc(q_ready, 1)

            def keys(p):
                has(act, km_dve_ready, p)
                for m in range(KC):
                    last = act.activation(k_t[:, m, :], kl_ps[0:DC, m * 2 * TOK:(m + 1) * 2 * TOK], ACT.Identity,
                                          bias=b_k[0:DC, m:m + 1])
                last.then_inc(k_ready, 1)

            def spread_keys(p, early):
                if early and p == 0:
                    act.wait_ge(const_a, HEAD_MASK)
                act.wait_ge(k_ready, p + 1)
                for h in range(ACT_HEADS):
                    last = act.activation(k_heads[:, :, :, h, :],
                                          k_t[:, :, :].rearrange("d m (b j) -> d m b j", j=TOK), ACT.Copy,
                                          scale=head_mask[:, h:h + 1])
                last.then_inc(km_act_ready, 1)

            def turned_norm2(p):
                act.wait_ge(xnt_done, p + 1)
                has(act, ll_done, p)
                act.activation(xn_t[:, :, 0:128], halves_of(qx_ps, 128), ACT.Copy).then_inc(xnt_ready, 1)

            def turned_probs(p):
                act.wait_ge(pta_done, p + 1)
                has(act, pv_done, p)
                turned = pt_ps[:, :, 0:HPC * 128].rearrange("p m (i q) -> p m i q", i=HPC)
                act.activation(probs_t[:, 0:HPC, :], turned[:, 0], ACT.Copy).then_inc(pta_ready, 1)
                act.wait_ge(ptb_done, p + 1)
                act.activation(probs_cls_t[:, :], pt_ps[0:HEADS, 1, HPC * 128:(HPC + 1) * 128], ACT.Copy)
                act.activation(probs_t[:, HPC:HP, :], turned[:, 1], ACT.Copy).then_inc(ptb_ready, 1)

            def routing(p):
                act.wait_ge(cmax_ready, p + 1)
                act.wait_ge(dmax_ready, p + 1)
                has(act, comb_ready, p)
                act.activation(c_exp[:, :], kl_ps[:, 0:NS], ACT.Exp, bias=c_max[:, 0:1],
                               accum_out=c_sum[:, 0:1]).then_inc(cexp_ready, 1)
                has(act, disp_ready, p)
                act.activation(d_exp[:, :], kl_ps[0:64, 64:64 + 129], ACT.Exp, bias=d_max[:, 0:1],
                               accum_out=d_sum[:, 0:1]).then_inc(dexp_ready, 1)

            def turned_weights(p):
                act.wait_ge(dc_done, p + 1)
                has(act, xx_done, p)
                act.activation(disp_t[:, :], qx_ps[:, 0:64], ACT.Copy).then_inc(dispt_ready, 1)
                act.activation(comb_t[:, p, :], qx_ps[:, 128:256], ACT.Copy).then_inc(combt_ready, 1)

            def turned_context(p, bank):
                act.wait_ge(ot_done, p + 1)
                has(act, wo_done, p)
                act.activation(ctx_t[:, :, :], halves_of(bank, 128), ACT.Copy).then_inc(ctxt_ready, 1)

            def turned_norm1(p):
                act.wait_ge(ln1t_done, p + 1)
                has(act, v_done, p)
                for k in range(KC):
                    last = act.activation(ln1_t[:, k, :, 1:TOK],
                                          o_ps[0:DC, k * 128:(k + 1) * 128].rearrange("p (b r) -> p b r", b=2),
                                          ACT.Copy)
                last.then_inc(ln1t_ready, 1)

            def slot_inputs(p):
                act.wait_ge(xx_done, p + 1)
                act.activation(slots_t[:, :, bass.ds(2 * p, 2), :].rearrange("d k b s -> d k (b s)"),
                               halves_of(vm_ps, 64), ACT.Copy).then_inc(slots_ready, 1)

            def slot(t, there):
                early = isinstance(t, int)
                if early and t == -2:
                    act.wait_ge(cls_step, CLS["ln_turned"])
                    act.activation(ln1_t[:, :, :, 0], halves_of(cls_ps, 64)[:, :, 0:2], ACT.Copy)
                    act.activation(cls_ln_t[:, :, :], halves_of(cls_ps, 64), ACT.Copy).then_inc(cls_step, 1)
                if there(0):
                    exponentials(t)
                if there(1):
                    queries(t + 1)
                    keys(t + 1)
                    if early and t == 0:
                        turned_probs(0)
                    spread_keys(t + 1, early)
                if early and t == -1:
                    act.wait_ge(cls_step, CLS["v_turned"])
                    act.activation(cls_v_t[:, :, :], halves_of(cls_ps, 64), ACT.Copy).then_inc(cls_step, 1)
                if there(-1):
                    turned_norm2(t - 1)
                if there(0) and not (early and t == 0):
                    turned_probs(t)
                if there(-1):
                    routing(t - 1)
                    turned_weights(t - 1)
                if early and t == 0:
                    act.wait_ge(cls_step, CLS["xn_turned"])
                    act.activation(cls_xn_t[:, :, :], halves_of(qx_ps, 64), ACT.Copy).then_inc(cls_step, 1)
                    act.activation(xn_t[:, :, 128:129], halves_of(qx_ps, 64)[:, :, 0:1], ACT.Copy)\
                       .then_inc(cls_xn_col, 1)
                if there(0):
                    turned_context(t, kl_ps)
                if there(2):
                    turned_norm1(t + 2)
                if there(-1):
                    slot_inputs(t - 1)

            def hidden_units(images):
                for n in range(EXPERTS):
                    g, j = divmod(n, 4)
                    rows = slice(32 * j, 32 * j + 32)
                    at = g * 64 + images.start * SLOTS
                    act.activation(hidden[rows, g, images.start:images.stop, n, :],
                                   hid_ps[rows, at:at + len(images) * SLOTS].rearrange("p (b s) -> p b s", s=SLOTS),
                                   ACT.Gelu, bias=b_down[rows, g:g + 1]).then_inc(hid_ready, 1)

            all_slots(act, slot)

            exponentials(PAIRS - 1)
            turned_probs(PAIRS - 1)
            turned_norm2(PAIRS - 2)
            act.wait_ge(cls_step, CLS["max"])
            act.activation(cc_exp[:, :], cls_end_ps[0:64, 0:NS], ACT.Exp, bias=cc_max[:, 0:1],
                           accum_out=cc_sum[:, 0:1]).then_inc(cls_step, 1)
            act.wait_ge(hid_done, 1)
            act.wait_ge(hidden_zero, 1)
            hidden_units(range(0, EARLY_IMAGES))
            turned_context(PAIRS - 1, qx_ps)
            load_table(ACT.Exp)
            routing(PAIRS - 2)
            turned_weights(PAIRS - 2)
            slot_inputs(PAIRS - 2)

            turned_norm2(PAIRS - 1)
            routing(PAIRS - 1)
            load_table(ACT.Gelu)
            turned_weights(PAIRS - 1)
            slot_inputs(PAIRS - 1)

            act.wait_ge(hid_done, 2)
            hidden_units(range(EARLY_IMAGES, B))
            act.wait_ge(y_ready, PAIRS - 1)
            act.dma_start(out_tok[:, PAIRS - 2, :], h_all[:, PAIRS - 2, :]).then_inc(out_act, 16)
            act.wait_ge(out_act, 16)


def _packed(np, fields, arrays, rows):
    got = np.zeros((rows, width(fields)), np.float32)
    at = 0
    for name, n in fields:
        a = arrays[name]
        got[:a.shape[0], at:at + n] = a.reshape(a.shape[0], n)
        at += n
    return got


def kernel(**inputs):
    import numpy as np
    import concourse.bacc as bacc
    from concourse.bass_utils import run_bass_kernel_spmd

    a = {k.removeprefix("L0_"): np.asarray(v) for k, v in inputs.items()}
    side = 8
    x = a["x"].reshape(PAIRS, 2, side, 16, side, 16, 3).transpose(0, 3, 5, 6, 1, 2, 4)
    x = x.reshape(PAIRS, PC, 128, 128).transpose(0, 2, 1, 3)
    wt = a["tok_W"].reshape(PC, 128, D).transpose(1, 0, 2)

    def rows(v, n=128):
        return np.broadcast_to(v.reshape(1, -1), (n, v.size))

    def chunks(w):
        return w.reshape(KC, DC, -1).transpose(1, 0, 2)

    def heads(w):
        return chunks(w.transpose(1, 0, 2).reshape(D, D))

    wdown = np.zeros((DC, KC, EXPERTS, QW), np.float32)
    wdown[:, :, :, :HID] = chunks(a["ffn_W_down"].transpose(1, 0, 2)).reshape(DC, KC, EXPERTS, HID)
    wup = np.zeros((4, QW, NG, D), np.float32)
    wup[:, :HID] = a["ffn_W_up"].reshape(NG, 4, HID, D).transpose(1, 2, 0, 3)
    bdown = np.zeros((4, QW, NG), np.float32)
    bdown[:, :HID] = a["ffn_b_down"].reshape(NG, 4, HID).transpose(1, 2, 0)
    bup = np.broadcast_to(a["ffn_b_up"][None, :, None, :], (4, EXPERTS, SLOTS, D)).reshape(128, D)
    pack_a = _packed(np, FIELDS_A, {
        "cls": rows(a["cls_tok"]), "btok": rows(a["tok_b"]), "bo": rows(a["attn_bo"]), "bv": rows(a["attn_bv"]),
        "bq": a["attn_bq"].reshape(KC, DC).T, "bk": a["attn_bk"].reshape(KC, DC).T,
        "scale": rows(a["ffn_scale"])}, 128)
    pack_b = _packed(np, FIELDS_B, {
        "wq": heads(a["attn_Wq"]), "wk": heads(a["attn_Wk"]), "wv": heads(a["attn_Wv"])}, DC)
    pack_c = _packed(np, FIELDS_C, {
        "wo": chunks(a["attn_Wo"]), "slots": chunks(a["ffn_slot_params"].reshape(D, NS)), "wdown": wdown,
        "wup": wup.reshape(128, NG * D), "bdown": bdown.reshape(128, NG), "bup": bup}, 128)

    nc = bacc.Bacc("TRN2", target_bir_lowering=False, num_devices=1)
    arrays, args = {}, []
    for name, v in (("xt", x), ("wtok", wt), ("pack_a", pack_a), ("pack_b", pack_b), ("pack_c", pack_c)):
        arrays[name] = np.ascontiguousarray(v)
        args.append(nc.dram_tensor(name, arrays[name].shape, F32, kind="ExternalInput").ap())
    args.append(nc.dram_tensor("out_tok", (128, PAIRS, D), F32, kind="ExternalOutput").ap())
    args.append(nc.dram_tensor("out_cls", (B, D), F32, kind="ExternalOutput").ap())
    vit_tower_kernel(nc, *args)
    r = run_bass_kernel_spmd(nc, [arrays], core_ids=[0])
    out = np.empty((B, TOK, D), np.float32)
    out[:, 0] = r.results[0]["out_cls"]
    out[:, 1:] = r.results[0]["out_tok"].transpose(1, 0, 2).reshape(B, NPATCH, D)
    return out
```

```python
from contextlib import ExitStack

import concourse.bass as bass
from concourse import mybir

F32 = mybir.dt.float32
BF16 = mybir.dt.bfloat16
ALU = mybir.AluOpType
ACT = mybir.ActivationFunctionType
AX = mybir.AxisListType

B, NPATCH, D, PIX = 16, 64, 192, 768
HEADS, HD = 12, 16
TOK = NPATCH + 1
EXPERTS, SLOTS, HID = 8, 4, 24
NS = EXPERTS * SLOTS
PAIRS = B // 2
KC = 2
DC = D // KC
PC = PIX // 128
HC = HEADS // KC
HP = HEADS // 2
HPC = HP // KC
VW = 2 * HD + 2
QW = 32
NG = EXPERTS // 4
GROUPS = B // 4
EARLY_IMAGES = B - 4
ACT_HEADS = 3
SM_SCALE = HD ** -0.5
LN_EPS = 1e-5
L2_EPS = 1e-6
MASKED = -1e30

FIELDS_A = [("cls", D), ("btok", D), ("bq", KC), ("bk", KC), ("scale", 1)]
FIELDS_B = [("wq", KC * D), ("wk", KC * D), ("wv", KC * D)]
FIELDS_D = [("bo", D), ("bv", D)]
FIELDS_C = [("wo", KC * D), ("slots", KC * NS), ("wdown", KC * EXPERTS * QW), ("wup", NG * D), ("bdown", NG), ("bup", D)]


def width(fields):
    return sum(n for _, n in fields)


def offsets(fields):
    at, out = 0, {}
    for name, n in fields:
        out[name] = (at, n)
        at += n
    return out


def vit_tower_kernel(nc, xt, wtok, pack_a, pack_b, pack_d, pack_c, out_tok, out_cls):
    with ExitStack() as ctx:
        def sb(name, shape, dt=F32):
            return ctx.enter_context(nc.sbuf_tensor(name, shape, dt))

        def sem(name):
            return ctx.enter_context(nc.semaphore(name))

        ident = sb("ident", [128, 128])
        ident_b = sb("ident_b", [128, 128], BF16)
        causal = sb("causal", [128, HC, TOK], BF16)
        slot_mask = sb("slot_mask", [64, 129], BF16)
        head_mask = sb("head_mask", [DC, HC])
        cls_head_mask = sb("cls_head_mask", [HEADS, HP, VW])
        cls_row_mask = sb("cls_row_mask", [128, GROUPS, B])
        powers = sb("powers", [128, 3])
        halves = sb("halves", [DC, KC, SLOTS])

        wt = sb("wt", [128, PC, D])
        pa = sb("pa", [128, width(FIELDS_A)])
        pb = sb("pb", [DC, width(FIELDS_B)])
        pc = sb("pc", [128, width(FIELDS_C)])
        pd = sb("pd", [128, width(FIELDS_D)])

        def field(name):
            for tile, fields in ((pa, FIELDS_A), (pb, FIELDS_B), (pc, FIELDS_C), (pd, FIELDS_D)):
                if name in offsets(fields):
                    a, n = offsets(fields)[name]
                    return tile[:, a:a + n]

        cls_in, b_tok, b_o, b_v = field("cls"), field("btok"), field("bo"), field("bv")
        b_q, b_k, slot_scale = field("bq"), field("bk"), field("scale")
        w_q = field("wq").rearrange("p (k n) -> p k n", k=KC)
        w_k = field("wk").rearrange("p (k n) -> p k n", k=KC)
        w_v = field("wv").rearrange("p (k n) -> p k n", k=KC)
        w_o = field("wo")[0:DC].rearrange("p (k n) -> p k n", k=KC)
        slots_in = field("slots")[0:DC].rearrange("p (k n) -> p k n", k=KC)
        w_down = field("wdown")[0:DC].rearrange("p (k e h) -> p k e h", k=KC, e=EXPERTS)
        w_up = field("wup").rearrange("p (g n) -> p g n", g=NG)
        b_down, b_up = field("bdown"), field("bup")

        slot_sq = sb("slot_sq", [DC, KC, NS])
        slot_ss = sb("slot_ss", [DC, KC, SLOTS])
        slot_inv = sb("slot_inv", [DC, KC, SLOTS])
        slot_dirs = sb("slot_dirs", [DC, KC, 2, NS])

        xt_first = sb("xt_first", [128, PC, 128])
        xt_next = sb("xt_next", [128, PC, 128])
        h_tok = sb("h_tok", [128, D])
        ln1_bn = sb("ln1_bn", [128, 6])
        ln1_mv = sb("ln1_mv", [128, 2])
        ln1_rstd = sb("ln1_rstd", [128, 2])
        ln1 = sb("ln1", [128, D])
        ln1_t = sb("ln1_t", [DC, KC, 2, TOK])
        q_t = sb("q_t", [DC, KC, 128])
        k_t = sb("k_t", [DC, KC, 2 * TOK])
        k_heads = sb("k_heads", [DC, KC, 2, HC, TOK])
        v_pairs = sb("v_pairs", [128, 2, HP, VW])
        s_max = sb("s_max", [128, HEADS])
        s_sub = sb("s_sub", [128, HEADS, TOK])
        probs = sb("probs", [128, HEADS, NPATCH])
        probs_cls = sb("probs_cls", [128, HEADS])
        probs_t = sb("probs_t", [128, HP, 128])
        probs_cls_t = sb("probs_cls_t", [HEADS, 128])
        p_inv = sb("p_inv", [128, HEADS])
        ctx_n = sb("ctx_n", [128, D])
        ctx_t = sb("ctx_t", [DC, KC, 128])
        ln2_bn = sb("ln2_bn", [128, 6])
        ln2_mv = sb("ln2_mv", [128, 2])
        ln2_s = sb("ln2_s", [128, 7])
        xn = sb("xn", [128, D])
        xn_last = sb("xn_last", [128, D])
        xn_t = sb("xn_t", [DC, KC, 129])
        c_max = sb("c_max", [128, 1])
        c_exp = sb("c_exp", [128, NS])
        c_sum = sb("c_sum", [128, 1])
        c_inv = sb("c_inv", [128, 1])
        comb = sb("comb", [128, 2, 2, NS])
        d_max = sb("d_max", [64, 1])
        d_exp = sb("d_exp", [64, 129])
        d_sum = sb("d_sum", [64, 1])
        d_inv = sb("d_inv", [64, 1])
        disp = sb("disp", [64, 129])
        disp_t = sb("disp_t", [128, 64])
        disp_cls = sb("disp_cls", [64, 64])

        h_all = sb("h_all", [128, PAIRS, D])
        comb_t = sb("comb_t", [128, PAIRS, 128])
        slots_t = sb("slots_t", [DC, KC, B, NS])
        hidden = sb("hidden", [128, NG, B, EXPERTS, SLOTS])
        y_slots = sb("y_slots", [128, GROUPS, D])

        c_bn = sb("c_bn", [64, 6])
        c_mv = sb("c_mv", [64, 2])
        c_rstd = sb("c_rstd", [64, 2])
        cls_ln = sb("cls_ln", [64, D])
        cls_ln_t = sb("cls_ln_t", [DC, KC, 64])
        cls_v = sb("cls_v", [64, D])
        cls_v_heads = sb("cls_v_heads", [HEADS, HP, VW])
        cls_v_t = sb("cls_v_t", [DC, KC, 64])
        cls_h = sb("cls_h", [64, D])
        c2_bn = sb("c2_bn", [64, 6])
        c2_mv = sb("c2_mv", [64, 2])
        c2_s = sb("c2_s", [64, 7])
        cls_xn = sb("cls_xn", [64, D])
        cls_xn_t = sb("cls_xn_t", [DC, KC, 64])
        cc_max = sb("cc_max", [64, 1])
        cc_exp = sb("cc_exp", [64, NS])
        cc_sum = sb("cc_sum", [64, 1])
        cc_inv = sb("cc_inv", [64, 1])
        cc = sb("cc", [64, 4, NS])
        cls_comb_t = sb("cls_comb_t", [128, GROUPS, B])
        cls_out = sb("cls_out", [B, D])
        idle = sb("idle", [128, 2 * 128], BF16)
        table = sb("table", [128, 4])

        bank = [ctx.enter_context(nc.psum_tensor(f"bank{i}", [128, 512], F32)) for i in (4, 5, 6, 7)]
        s_ps = ctx.enter_context(nc.psum_tensor("s_ps", [128, KC, 512], F32))
        pt_ps = ctx.enter_context(nc.psum_tensor("pt_ps", [128, 2, 512], F32))
        qx_ps, kl_ps, vm_ps, o_ps = bank
        cls_ps = pt_ps[:, 0, :]
        cls_end_ps = s_ps[:, 1, :]
        tok_first_ps, tok_second_ps = vm_ps, s_ps[:, 0, :]
        hid_ps = s_ps[:, 0, :]
        ys_bank = [s_ps[:, 1, :], pt_ps[:, 0, :], pt_ps[:, 1, :], vm_ps]
        y_bank = [o_ps, pt_ps[:, 0, :], pt_ps[:, 1, :]]
        yc_ps = s_ps[:, 1, :]
        last_context_ps, last_norm2_ps = pt_ps[:, 0, :], pt_ps[:, 1, :]

        in_next, in_a, in_b, in_c, in_d = (sem(n) for n in ("in_next", "in_a", "in_b", "in_c", "in_d"))
        in_first, in_wt = [sem("in_first_0"), sem("in_first_1")], [sem("in_wt_0"), sem("in_wt_1")]
        const_a, hidden_zero, slot_step, cls_step = (sem(n) for n in ("const_a", "hidden_zero", "slot_step", "cls_step"))
        idle_ready, cls_values, cls_bo, cls_xn_col, slot_inv_ready = (sem(n) for n in (
            "idle_ready", "cls_values", "cls_bo", "cls_xn_col", "slot_inv_ready"))
        (tok_done, ln1t_done, qk_done, v_done, s_done, pta_done, ptb_done, pv_done, ot_done, wo_done, xnt_done,
         ll_done, dc_done, xx_done) = (sem(n) for n in (
             "tok_done", "ln1t_done", "qk_done", "v_done", "s_done", "pta_done", "ptb_done", "pv_done", "ot_done",
             "wo_done", "xnt_done", "ll_done", "dc_done", "xx_done"))
        (h_ready, hbo_ready, ln1_step, ln1t_ready, q_ready, k_ready, km_act_ready, km_dve_ready, v_ready, smax_ready, ssub_ready,
         probs_ready, pta_ready, ptb_ready, pinv_ready, ctx_ready, ctxt_ready, h1_ready, ln2_step, xnt_ready,
         cmax_ready, cexp_ready, cinv_ready, comb_ready, dmax_ready, dexp_ready, dinv_ready, disp_ready,
         dcls_ready, dispt_ready, combt_ready, slots_ready) = (sem(n) for n in (
             "h_ready", "hbo_ready", "ln1_step", "ln1t_ready", "q_ready", "k_ready", "km_act_ready", "km_dve_ready",
             "v_ready",
             "smax_ready", "ssub_ready", "probs_ready", "pta_ready", "ptb_ready", "pinv_ready", "ctx_ready",
             "ctxt_ready", "h1_ready", "ln2_step", "xnt_ready", "cmax_ready", "cexp_ready", "cinv_ready",
             "comb_ready", "dmax_ready", "dexp_ready", "dinv_ready", "disp_ready", "dcls_ready", "dispt_ready",
             "combt_ready", "slots_ready"))
        passed = sem("passed")
        hid_done, hid_ready, ys_done, ys_ready, y_done, y_ready, yc_done, yc_ready, out_sp, out_act = (sem(n) for n in (
            "hid_done", "hid_ready", "ys_done", "ys_ready", "y_done", "y_ready", "yc_done", "yc_ready",
            "out_sp", "out_act"))
        SLOT_STEPS = 10
        WAIT_INPUTS, WAIT_NORM1, WAIT_COPY, WAIT_SOFTMAX, WAIT_ROUTING = 15, 8, 6, 10, 10
        IDENT, POWERS, HEAD_MASK, CAUSAL, CLS_HEADS, SLOT_MASK, CONSTANTS = 2, 5, 8, 12, 15, 18, 23
        LN1_STEPS, LN2_STEPS = 5, 7
        names = ("stats mean var_eps rstd ln ln_turned ln_t v_ps v v_heads v_turned v_t wo_ps h".split()
                 + [f"norm2_{i}" for i in range(1, LN2_STEPS)]
                 + "xn xn_turned xn_t logits max exp inv comb comb_turned comb_t".split())
        CLS = {name: i + 1 for i, name in enumerate(names)}

        def has(eng, s, n):
            if not isinstance(n, int) or n > 0:
                eng.wait_ge(s, n)

        def settled(eng):
            eng.sem_inc(passed, 1)

        def capped(n):
            return min(n, PAIRS) if isinstance(n, int) else n

        def all_slots(eng, run):
            run(1)
            with eng.Fori(2, PAIRS - 2) as t:
                run(t)

        PC_PARTS = [slice(0, PC // 2), slice(PC // 2, PC)]

        EARLY_CHUNKS = 4

        block = ctx.enter_context(nc.Block())

        @block.sync
        def _(sp):
            for i, part in enumerate(PC_PARTS):
                sp.dma_start(wt[:, part, :], wtok[:, part, :]).then_inc(in_wt[i], 16)
            sp.dma_start(pa[:, :], pack_a).then_inc(in_a, 16)
            sp.dma_start(pb[:, :], pack_b).then_inc(in_b, 16)
            sp.dma_start(pc[:, :], pack_c).then_inc(in_c, 16)
            with sp.Fori(2, PAIRS) as p:
                sp.wait_ge(tok_done, p)
                sp.dma_start(xt_next[:, :, :], xt[p]).then_inc(in_next, 16)
            for first, end in ((0, 3), (3, PAIRS - 2), (PAIRS - 1, PAIRS)):
                sp.wait_ge(y_ready, end)
                sp.dma_start(out_tok[:, first:end, :], h_all[:, first:end, :]).then_inc(out_sp, 16)
            sp.wait_ge(yc_ready, 1)
            sp.dma_start(out_cls, cls_out[:, :]).then_inc(out_sp, 16)
            sp.wait_ge(out_sp, 16 * 4)

        @block.gpsimd
        def _(pool):
            made = [0]

            def then(instruction):
                made[0] += 1
                instruction.then_inc(const_a, 1)
                pool.wait_ge(const_a, made[0])

            def keep(tile, compare, fill, base, pattern, channel):
                then(pool.affine_select(out=tile, in_=tile, compare_op=compare, fill=fill, base=base,
                                        pattern=pattern, channel_multiplier=channel))

            then(pool.memset(ident[:, :], 0.0))
            keep(ident[:, :], ALU.not_equal, 1.0, 0, [[-1, 128]], 1)
            then(pool.memset(powers[:, 0:1], -0.5))
            then(pool.memset(powers[:, 1:3], 0.5))
            then(pool.memset(halves[:, :, :], 0.5))
            then(pool.memset(head_mask[:, :], 1.0))
            keep(head_mask[:, :], ALU.is_ge, 0.0, 0, [[-HD, HC]], 1)
            keep(head_mask[:, :], ALU.is_ge, 0.0, HD - 1, [[HD, HC]], -1)
            then(pool.tensor_copy(ident_b[:, :], ident[:, :]))
            then(pool.memset(causal[:, :, :], 0.0))
            for b in range(2):
                keep(causal[64 * b:64 * b + 64], ALU.is_ge, MASKED, 1, [[0, HC], [-1, TOK]], 1)
            then(pool.memset(cls_head_mask[:, :, :], 1.0))
            keep(cls_head_mask[:, :, 0:2 * HD].rearrange("h p (e d) -> h p e d", e=2), ALU.is_equal, 0.0, 0,
                 [[-2, HP], [-1, 2], [0, HD]], 1)
            keep(cls_head_mask[:, :, 2 * HD:VW], ALU.is_equal, 0.0, 0, [[-2, HP], [-1, 2]], 1)

            def late_masks():
                then(pool.memset(slot_mask[:, :], 0.0))
                for b in range(2):
                    then(pool.memset(slot_mask[NS * b:NS * b + NS, 64 * (1 - b):64 * (1 - b) + 64], MASKED))
                then(pool.memset(cls_row_mask[:, :, :], 1.0))
                for b in range(4):
                    keep(cls_row_mask[NS * b:NS * b + NS], ALU.is_equal, 0.0, -b, [[-4, GROUPS], [1, B]], 0)
                assert made[0] == CONSTANTS

            def power(dst, src, exponents, step, n):
                pool.wait_ge(step, n)
                pool.tensor_tensor(dst, src, exponents, ALU.pow).then_inc(step, 1)

            def norm1_power(p):
                power(ln1_rstd[:, 1:2], ln1_rstd[:, 0:1], powers[:, 0:1], ln1_step, LN1_STEPS * p + 3)

            def residual(p):
                pool.wait_ge(h_ready, p + 1)
                pool.tensor_tensor(h_all[:, p, :], h_tok[:, :], b_o, ALU.add).then_inc(hbo_ready, 1)

            def norm2_powers(p):
                power(ln2_s[:, 2:4], ln2_s[:, 0:2], powers[:, 1:3], ln2_step, LN2_STEPS * p + 3)

            def cls_share(p):
                pool.wait_ge(disp_ready, p + 1)
                has(pool, xx_done, p)
                settled(pool)
                pool.tensor_scalar(disp_cls[:, :], ident[0:64, 0:64], disp[:, 128:129], None,
                                   ALU.mult).then_inc(dcls_ready, 1)

            def slot(t):
                norm2_powers(t - 1)
                norm1_power(t + 2)
                residual(t + 2)
                cls_share(t - 1)

            norm1_power(0)
            power(c_rstd[:, 1:2], c_rstd[:, 0:1], powers[0:64, 0:1], cls_step, CLS["var_eps"])
            pool.wait_ge(in_d, 16)
            residual(0)
            norm1_power(1)
            residual(1)
            late_masks()
            power(slot_ss[:, :, :], slot_ss[:, :, :], halves[:, :, :], slot_step, 6)
            power(c2_s[:, 2:4], c2_s[:, 0:2], powers[0:64, 1:3], cls_step, CLS["norm2_3"])
            norm1_power(2)
            residual(2)

            all_slots(pool, slot)

            norm2_powers(PAIRS - 3)
            norm2_powers(PAIRS - 2)
            cls_share(PAIRS - 3)
            norm2_powers(PAIRS - 1)
            cls_share(PAIRS - 2)
            cls_share(PAIRS - 1)

        @block.tensor
        def _(pe):
            mm, tr = pe.matmul, pe.transpose

            def two_transposes(dst, src, rows):
                for kc in range(KC):
                    last = tr(dst[0:DC, kc * rows:(kc + 1) * rows], src[0:rows, kc * DC:(kc + 1) * DC],
                              ident[0:rows, 0:rows])
                return last

            def two_chunks(dst, lhs, rhs, first=True):
                for kc in range(KC):
                    last = mm(dst, lhs(kc), rhs(kc), start=first and kc == 0, stop=kc == KC - 1)
                return last

            def keep_clock(n, bank):
                for _ in range(n):
                    mm(bank[:, 0:2 * 128], idle[:, 0:128], idle[:, :], start=True, stop=True)

            def cls_part(result):
                if result == "ln_turned":
                    pe.wait_ge(cls_step, CLS["ln"])
                    two_transposes(cls_ps, cls_ln, 64).then_inc(cls_step, 1)
                if result == "v_ps":
                    pe.wait_ge(cls_step, CLS["ln_t"])
                    two_chunks(cls_ps[0:64, 0:D], lambda k: cls_ln_t[:, k, :], lambda k: w_v[:, k, :])\
                        .then_inc(cls_step, 1)
                if result == "v_turned":
                    pe.wait_ge(cls_step, CLS["v_heads"])
                    two_transposes(cls_ps, cls_v, 64).then_inc(cls_step, 1)
                if result == "wo_ps":
                    pe.wait_ge(in_c, 16)
                    pe.wait_ge(cls_step, CLS["v_t"])
                    two_chunks(cls_ps[0:64, 0:D], lambda k: cls_v_t[:, k, :], lambda k: w_o[:, k, :])\
                        .then_inc(cls_step, 1)
                if result == "xn_turned":
                    pe.wait_ge(cls_step, CLS["xn"])
                    pe.wait_ge(q_ready, 2)
                    two_transposes(qx_ps, cls_xn, 64).then_inc(cls_step, 1)
                if result == "logits":
                    two_chunks(cls_end_ps[0:64, 0:NS], lambda k: cls_xn_t[:, k, :], lambda k: slot_dirs[:, k, 0, :])\
                        .then_inc(cls_step, 1)
                if result == "comb_turned":
                    pe.wait_ge(cls_step, CLS["comb"])
                    tr(cls_end_ps[:, 0:64], cc[:, :, :].rearrange("p b s -> p (b s)"), ident[0:64, 0:64])\
                        .then_inc(cls_step, 1)

            def queries_and_keys(p, early):
                if early:
                    pe.wait_ge(ln1t_ready, p + 1)
                    has(pe, combt_ready, p - 2)
                    has(pe, ctxt_ready, p - 1)
                for m in range(KC):
                    q_rhs = lambda k: ln1_t[:, k, :, 1:TOK]
                    k_rhs = lambda k: ln1_t[:, k, :, :]
                    two_chunks(qx_ps[0:DC, m * 128:(m + 1) * 128], lambda k: w_q[:, k, m * DC:(m + 1) * DC], q_rhs)
                    last = two_chunks(kl_ps[0:DC, m * 2 * TOK:(m + 1) * 2 * TOK],
                                      lambda k: w_k[:, k, m * DC:(m + 1) * DC], k_rhs)
                last.then_inc(qk_done, 1)

            def embedding(p, bank, first=False, chunks=range(PC)):
                if chunks.start == 0:
                    if not first:
                        pe.wait_ge(in_next, 16 * p)
                    has(pe, slots_ready, p - 3)
                    has(pe, v_ready, p - 1)
                x = xt_first if first else xt_next
                for c in chunks:
                    for i, part in enumerate(PC_PARTS):
                        if first and c == part.start:
                            pe.wait_ge(in_wt[i], 16)
                            pe.wait_ge(in_first[i], 16)
                    last = mm(bank[:, 0:D], x[:, c, :], wt[:, c, :], start=c == 0, stop=c == PC - 1)
                if chunks.stop == PC:
                    last.then_inc(tok_done, 1)

            def values(p):
                has(pe, h_ready, capped(p + 2))
                two_chunks(vm_ps[0:64, 0:D], lambda k: ln1_t[:, k, 0, 1:TOK], lambda k: w_v[:, k, :])
                two_chunks(vm_ps[64:128, 0:D], lambda k: ln1_t[:, k, 1, 1:TOK], lambda k: w_v[:, k, :])\
                    .then_inc(v_done, 1)

            def scores(p, m, early):
                if m == 0:
                    if early and p == 0:
                        pe.wait_ge(const_a, CAUSAL)
                    pe.wait_ge(km_act_ready, p + 1)
                    pe.wait_ge(km_dve_ready, p + 1)
                has(pe, ssub_ready, KC * (p - 1) + m + 1)
                dst = s_ps[:, m, 0:HC * TOK]
                mm(dst, ident_b[:, :], causal[:, :, :].rearrange("p h j -> p (h j)"), start=True, stop=False,
                   skip_group_check=True)
                for b in range(2):
                    last = mm(s_ps[64 * b:64 * b + 64, m, 0:HC * TOK], q_t[:, m, 64 * b:64 * b + 64],
                              k_heads[:, m, b, :, :].rearrange("d h j -> d (h j)"), start=False, stop=True,
                              skip_group_check=True)
                last.then_inc(s_done, 1)

            def turn_probs(p):
                for m, turned in enumerate((pta_done, ptb_done)):
                    pe.wait_ge(probs_ready, KC * p + m + 1)
                    for i in range(HPC):
                        h = m * HC + 2 * i
                        last = tr(pt_ps[:, m, i * 128:(i + 1) * 128],
                                  probs[:, h:h + 2, :].rearrange("p h j -> p (h j)"), ident[:, :])
                    if m == KC - 1:
                        last = tr(pt_ps[0:HEADS, m, HPC * 128:(HPC + 1) * 128], probs_cls[:, :], ident[:, :])
                    last.then_inc(turned, 1)

            def context(p, early):
                pe.wait_ge(ptb_ready, p + 1)
                if early:
                    has(pe, h1_ready, p)
                    pe.wait_ge(v_ready, p + 1)
                if early and p == 0:
                    pe.wait_ge(cls_values, 1)
                mm(o_ps[:, 0:HP * VW], probs_cls_t[:, :], cls_v_heads[:, :, :].rearrange("h p w -> h (p w)"),
                   start=True, stop=False, skip_group_check=True)
                for i in range(HP):
                    for b in range(2):
                        last = mm(o_ps[64 * b:64 * b + 64, i * VW:(i + 1) * VW],
                                  probs_t[:, i, 64 * b:64 * b + 64], v_pairs[:, b, i, :],
                                  start=False, stop=True, skip_group_check=True)
                last.then_inc(pv_done, 1)

            def turn_context(p, bank):
                pe.wait_ge(ctx_ready, p + 1)
                two_transposes(bank, ctx_n, 128).then_inc(ot_done, 1)

            def turn_norm1(p):
                pe.wait_ge(ln1_step, LN1_STEPS * (p + 1))
                has(pe, ctx_ready, p - 1)
                two_transposes(o_ps, ln1, 128).then_inc(ln1t_done, 1)

            def projection(p, early):
                has(pe, ln1t_ready, capped(p + 3))
                if early:
                    pe.wait_ge(ctxt_ready, p + 1)
                two_chunks(o_ps[:, 0:D], lambda k: ctx_t[:, k, :], lambda k: w_o[:, k, :]).then_inc(wo_done, 1)

            def turn_norm2(p, tokens, bank):
                pe.wait_ge(ln2_step, LN2_STEPS * (p + 1))
                has(pe, q_ready, capped(p + 3))
                two_transposes(bank, tokens, 128).then_inc(xnt_done, 1)

            def logits(p, early):
                pe.wait_ge(xnt_ready, p + 1)
                if early:
                    has(pe, k_ready, capped(p + 3))
                if early and p == 0:
                    pe.wait_ge(cls_xn_col, 1)
                    pe.wait_ge(const_a, SLOT_MASK)
                    pe.wait_ge(slot_step, SLOT_STEPS)
                two_chunks(kl_ps[:, 0:NS], lambda k: xn_t[:, k, 0:128], lambda k: slot_dirs[:, k, 0, :])
                mm(kl_ps[0:64, 64:64 + 129], ident_b[0:64, 0:64], slot_mask[:, :], start=True, stop=False)
                two_chunks(kl_ps[0:64, 64:64 + 129],
                           lambda k: slot_dirs[:, k, :, :].rearrange("p b s -> p (b s)"),
                           lambda k: xn_t[:, k, :], first=False).then_inc(ll_done, 1)

            def turn_weights(p):
                pe.wait_ge(disp_ready, p + 1)
                settled(pe)
                tr(qx_ps[:, 128:256], comb[:, :, :, :].rearrange("p c b s -> p (c b s)"), ident[:, :])
                tr(qx_ps[:, 0:64], disp[:, 0:128], ident[0:64, 0:64]).then_inc(dc_done, 1)

            def slot_inputs(p, tokens):
                pe.wait_ge(dispt_ready, p + 1)
                pe.wait_ge(dcls_ready, p + 1)
                has(pe, v_ready, capped(p + 3))
                for kc in range(KC):
                    mm(vm_ps[0:DC, kc * 64:(kc + 1) * 64], tokens[:, kc * DC:(kc + 1) * DC], disp_t[:, :],
                       start=True, stop=False)
                    last = mm(vm_ps[0:DC, kc * 64:(kc + 1) * 64], cls_xn[:, kc * DC:(kc + 1) * DC],
                              disp_cls[:, :], start=False, stop=True)
                last.then_inc(xx_done, 1)

            def slot(t):
                early = isinstance(t, int)
                if early and t == 1:
                    pe.wait_ge(cls_xn_col, 1)
                queries_and_keys(t + 1, early)
                embedding(t + 2, vm_ps)
                turn_norm2(t - 1, xn, qx_ps)
                turn_probs(t)
                logits(t - 1, early)
                context(t, early)
                values(t + 1)
                scores(t + 1, 0, early)
                turn_weights(t - 1)
                turn_context(t, kl_ps)
                turn_norm1(t + 2)
                scores(t + 1, 1, early)
                slot_inputs(t - 1, xn)
                projection(t, early)

            def hidden_units(images):
                for n in range(EXPERTS):
                    g, j = divmod(n, 4)
                    at = g * 64 + images.start * SLOTS
                    last = two_chunks(hid_ps[32 * j:32 * j + 32, at:at + len(images) * SLOTS],
                                      lambda k: w_down[:, k, n, :],
                                      lambda k: slots_t[:, k, images.start:images.stop, n * SLOTS:(n + 1) * SLOTS])
                last.then_inc(hid_done, 1)

            def slot_outputs(c):
                for g in range(NG):
                    if c == GROUPS - 1:
                        pe.wait_ge(hid_ready, EXPERTS + 4 * (g + 1))
                    last = mm(ys_bank[c][:, 0:D],
                              hidden[:, g, 4 * c:4 * c + 4, :, :].rearrange("p b e s -> p (b e s)"),
                              w_up[:, g, :], start=g == 0, stop=g == NG - 1)
                last.then_inc(ys_done, 1)

            def token_outputs(p):
                pe.wait_ge(combt_ready, p + 1)
                if p == 0:
                    pe.wait_ge(h1_ready, PAIRS)
                pe.wait_ge(ys_ready, max(p // 2 + 1, min(p + 1, len(y_bank))))
                has(pe, y_ready, p + 1 - len(y_bank))
                half = slice(64 * (p % 2), 64 * (p % 2) + 64)
                mm(y_bank[p % 3][:, 0:D], comb_t[half, p, :], y_slots[half, p // 2, :], start=True, stop=True)\
                    .then_inc(y_done, 1)

            def cls_outputs(c):
                pe.wait_ge(ys_ready, c + 1)
                last = mm(yc_ps[0:B, 0:D], cls_comb_t[:, c, :], y_slots[:, c, :], start=c == 0, stop=c == GROUPS - 1)
                if c == GROUPS - 1:
                    last.then_inc(yc_done, 1)

            pe.wait_ge(idle_ready, 1)
            keep_clock(WAIT_INPUTS, vm_ps)
            embedding(0, tok_first_ps, True)
            embedding(1, tok_second_ps)
            keep_clock(WAIT_NORM1, qx_ps)
            pe.wait_ge(const_a, IDENT)
            turn_norm1(0)
            cls_part("ln_turned")
            keep_clock(WAIT_COPY, qx_ps)
            pe.wait_ge(cls_step, CLS["ln_t"])
            pe.wait_ge(in_b, 16)
            queries_and_keys(0, True)
            turn_norm1(1)
            values(0)
            cls_part("v_ps")
            pe.wait_ge(q_ready, 1)
            pe.wait_ge(k_ready, 1)
            queries_and_keys(1, True)
            cls_part("v_turned")
            scores(0, 0, True)
            scores(0, 1, True)
            cls_part("wo_ps")
            embedding(2, vm_ps, chunks=range(0, EARLY_CHUNKS))
            pe.wait_ge(cls_bo, 1)
            turn_probs(0)
            embedding(2, vm_ps, chunks=range(EARLY_CHUNKS, PC))
            context(0, True)
            values(1)
            scores(1, 0, True)
            turn_context(0, kl_ps)
            cls_part("xn_turned")
            turn_norm1(2)
            scores(1, 1, True)
            projection(0, True)

            all_slots(pe, slot)

            queries_and_keys(PAIRS - 1, True)
            turn_probs(PAIRS - 2)
            pe.wait_ge(slots_ready, PAIRS - 3)
            pe.wait_ge(v_ready, PAIRS - 1)
            keep_clock(WAIT_COPY, vm_ps)
            turn_norm2(PAIRS - 3, xn, qx_ps)
            context(PAIRS - 2, True)
            values(PAIRS - 1)
            scores(PAIRS - 1, 0, True)
            scores(PAIRS - 1, 1, True)
            turn_context(PAIRS - 2, last_context_ps)
            logits(PAIRS - 3, True)
            projection(PAIRS - 2, True)

            pe.wait_ge(ssub_ready, KC * PAIRS)
            cls_part("logits")
            turn_probs(PAIRS - 1)
            pe.wait_ge(v_ready, PAIRS)
            keep_clock(WAIT_SOFTMAX, vm_ps)
            context(PAIRS - 1, True)
            turn_weights(PAIRS - 3)
            turn_norm2(PAIRS - 2, xn_last, last_norm2_ps)
            turn_context(PAIRS - 1, last_context_ps)
            logits(PAIRS - 2, True)
            projection(PAIRS - 1, True)
            cls_part("comb_turned")
            slot_inputs(PAIRS - 3, xn)
            pe.wait_ge(slots_ready, EARLY_IMAGES // 2)
            hidden_units(range(0, EARLY_IMAGES))
            keep_clock(WAIT_ROUTING, vm_ps)
            turn_weights(PAIRS - 2)

            turn_norm2(PAIRS - 1, xn, last_norm2_ps)
            logits(PAIRS - 1, True)
            slot_inputs(PAIRS - 2, xn_last)
            pe.wait_ge(cls_step, CLS["comb_t"])
            pe.wait_ge(hid_ready, EXPERTS)
            slot_outputs(0)
            slot_outputs(1)
            turn_weights(PAIRS - 1)
            slot_outputs(2)
            pe.wait_ge(slots_ready, PAIRS - 1)
            slot_inputs(PAIRS - 1, xn)
            token_outputs(0)

            pe.wait_ge(slots_ready, PAIRS)
            hidden_units(range(EARLY_IMAGES, B))
            for p in range(1, EARLY_IMAGES // 2):
                token_outputs(p)
            slot_outputs(GROUPS - 1)
            for c in range(GROUPS - 1):
                cls_outputs(c)
            token_outputs(PAIRS - 2)
            token_outputs(PAIRS - 1)
            cls_outputs(GROUPS - 1)

        @block.vector
        def _(dve):
            dve.memset(table[:, :], 0.0)
            dve.memset(idle[:, :], 0.0).then_inc(idle_ready, 1)
            dve.memset(v_pairs[:, :, :, :], 0.0).then_inc(slot_step, 1)
            dve.memset(comb[:, :, :, :], 0.0).then_inc(slot_step, 1)
            dve.memset(hidden[:, :, :, :, :], 0.0).then_inc(hidden_zero, 1)
            dve.wait_ge(slot_step, 2)
            dve.memset(v_pairs[0:64, :, :, 2 * HD:2 * HD + 1], 1.0).then_inc(slot_step, 1)
            dve.memset(v_pairs[64:128, :, :, 2 * HD + 1:VW], 1.0).then_inc(slot_step, 1)

            def cls_statistics():
                dve.bn_stats(c_bn[:, :], cls_in[0:64]).then_inc(cls_step, 1)
                dve.wait_ge(cls_step, CLS["stats"])
                dve.bn_aggr(c_mv[:, :], c_bn[:, :]).then_inc(cls_step, 1)
                dve.wait_ge(cls_step, CLS["mean"])
                dve.tensor_scalar(c_rstd[:, 0:1], c_mv[:, 1:2], LN_EPS, None, ALU.add).then_inc(cls_step, 1)

            def cls_norm():
                dve.wait_ge(cls_step, CLS["rstd"])
                dve.tensor_scalar(cls_ln[:, :], cls_in[0:64], c_mv[:, 0:1], c_rstd[:, 1:2], ALU.subtract, ALU.mult)\
                   .then_inc(cls_step, 1)

            def cls_value():
                dve.wait_ge(in_d, 16)
                dve.wait_ge(cls_step, CLS["v_ps"])
                dve.tensor_tensor(cls_v[:, :], cls_ps[0:64, 0:D], b_v[0:64], ALU.add).then_inc(cls_step, 1)
                dve.wait_ge(cls_step, CLS["v"])
                dve.tensor_copy(cls_v_heads[:, :, 0:2 * HD], cls_v[0:HEADS].rearrange("h (p w) -> h p w", p=HP))\
                   .then_inc(cls_step, 1)
                dve.wait_ge(cls_step, CLS["v_heads"])
                dve.wait_ge(const_a, CLS_HEADS)
                dve.tensor_tensor(cls_v_heads[:, :, 0:2 * HD], cls_v_heads[:, :, 0:2 * HD],
                                  cls_head_mask[:, :, 0:2 * HD], ALU.mult)
                dve.tensor_copy(cls_v_heads[:, :, 2 * HD:VW], cls_head_mask[:, :, 2 * HD:VW])\
                   .then_inc(cls_values, 1)

            def norm2_variance(bn, mv, s, src, step, base):
                settled(dve)
                dve.bn_stats(bn[:, :], src).then_inc(step, 1)
                dve.wait_ge(step, base + 1)
                settled(dve)
                dve.bn_aggr(mv[:, :], bn[:, :]).then_inc(step, 1)
                dve.wait_ge(step, base + 2)
                dve.tensor_scalar(s[:, 0:1], mv[:, 1:2], LN_EPS, None, ALU.add)
                dve.tensor_scalar(s[:, 1:2], mv[:, 1:2], float(D), None, ALU.mult).then_inc(step, 1)

            def norm2_scaled(mv, s, src, dst, step, base):
                dve.wait_ge(step, base + 4)
                dve.tensor_scalar(s[:, 4:5], s[:, 2:3], L2_EPS, s[:, 3:4], ALU.mult, ALU.add).then_inc(step, 1)
                dve.wait_ge(step, base + 5)
                dve.reciprocal(s[:, 5:6], s[:, 4:5]).then_inc(step, 1)
                dve.wait_ge(step, base + 6)
                dve.tensor_scalar(dst, src, mv[:, 0:1], s[:, 5:6], ALU.subtract, ALU.mult).then_inc(step, 1)

            def cls_output():
                dve.wait_ge(cls_step, CLS["wo_ps"])
                dve.tensor_tensor(cls_h[:, :], cls_ps[0:64, 0:D], b_o[0:64], ALU.add).then_inc(cls_bo, 1)
                dve.wait_ge(cls_bo, 1)
                dve.tensor_tensor(cls_h[:, :], cls_h[:, :], cls_in[0:64], ALU.add).then_inc(cls_step, 1)
                dve.wait_ge(cls_step, CLS["h"])
                norm2_variance(c2_bn, c2_mv, c2_s, cls_h[:, :], cls_step, CLS["h"])

            def cls_norm2():
                norm2_scaled(c2_mv, c2_s, cls_h[:, :], cls_xn[:, :], cls_step, CLS["h"])

            def cls_largest_logit():
                dve.wait_ge(cls_step, CLS["logits"])
                dve.tensor_reduce(cc_max[:, :], cls_end_ps[0:64, 0:NS], AX.X, ALU.max, negate=True)\
                   .then_inc(cls_step, 1)

            def cls_weights():
                dve.wait_ge(cls_step, CLS["exp"])
                dve.reciprocal(cc_inv[:, :], cc_sum[:, :]).then_inc(cls_step, 1)
                dve.wait_ge(cls_step, CLS["inv"])
                dve.tensor_scalar(cc[:, :, :], cc_exp[:, :].unsqueeze(1).to_broadcast([64, 4, NS]), cc_inv[:, 0:1], None,
                                  ALU.mult).then_inc(cls_step, 1)

            def cls_rows():
                dve.wait_ge(cls_step, CLS["comb_turned"])
                dve.wait_ge(const_a, CONSTANTS)
                dve.tensor_scalar(cls_comb_t[:, :, :], cls_row_mask[:, :, :], cls_end_ps[:, 0:1], None, ALU.mult)\
                   .then_inc(cls_step, 1)

            def slot_squares():
                dve.wait_ge(in_c, 16)
                dve.tensor_tensor(slot_sq[:, :, :], slots_in, slots_in, ALU.mult).then_inc(slot_step, 1)
                dve.wait_ge(slot_step, 5)
                dve.tensor_reduce(slot_ss[:, :, :], slot_sq[:, :, :].rearrange("d k (n s) -> d k s n", s=SLOTS),
                                  AX.X, ALU.add).then_inc(slot_step, 1)

            def slot_directions():
                dve.wait_ge(slot_step, 7)
                dve.tensor_scalar(slot_ss[:, :, :], slot_ss[:, :, :], L2_EPS, None, ALU.add).then_inc(slot_step, 1)
                dve.wait_ge(slot_step, 8)
                dve.reciprocal(slot_inv[:, :, :], slot_ss[:, :, :]).then_inc(slot_step, 1)
                dve.wait_ge(slot_step, 9)
                dve.tensor_scalar(slot_inv[:, :, :], slot_inv[:, :, :], slot_scale[0:DC], None, ALU.mult)\
                   .then_inc(slot_inv_ready, 1)
                dve.wait_ge(slot_inv_ready, 1)
                for k in range(KC):
                    for b in range(2):
                        last = dve.tensor_tensor(
                            slot_dirs[:, k, b, :].rearrange("d (n s) -> d n s", s=SLOTS),
                            slots_in[:, k, :].rearrange("d (n s) -> d n s", s=SLOTS),
                            slot_inv[:, k, :].unsqueeze(1).to_broadcast([DC, EXPERTS, SLOTS]), ALU.mult)
                last.then_inc(slot_step, 1)

            def largest_scores(p):
                src = s_ps[:, :, 0:HC * TOK].rearrange("p m (h j) -> p m h j", j=TOK)
                for m in range(KC):
                    dve.wait_ge(s_done, KC * p + m + 1)
                    dve.tensor_reduce(s_max[:, m * HC:(m + 1) * HC], src[:, m], AX.X, ALU.max).then_inc(smax_ready, 1)
                for m in range(KC):
                    dve.wait_ge(smax_ready, KC * p + m + 1)
                    has(dve, probs_ready, KC * (p - 1) + m + 1)
                    dve.tensor_tensor(
                        s_sub[:, m * HC:(m + 1) * HC, :], src[:, m],
                        s_max[:, m * HC:(m + 1) * HC].unsqueeze(2).to_broadcast([128, HC, TOK]), ALU.subtract)\
                       .then_inc(ssub_ready, 1)

            def residual_and_variance(p):
                dve.wait_ge(wo_done, p + 1)
                dve.wait_ge(hbo_ready, p + 1)
                dve.tensor_tensor(h_all[:, p, :], o_ps[:, 0:D], h_all[:, p, :], ALU.add).then_inc(h1_ready, 1)
                dve.wait_ge(h1_ready, p + 1)
                norm2_variance(ln2_bn, ln2_mv, ln2_s, h_all[:, p, :], ln2_step, LN2_STEPS * p)

            def norm2(p, tokens, used):
                has(dve, xx_done, used)
                norm2_scaled(ln2_mv, ln2_s, h_all[:, p, :], tokens[:, :], ln2_step, LN2_STEPS * p)

            def spread_keys(p, early):
                dve.wait_ge(k_ready, p + 1)
                has(dve, s_done, KC * p)
                if early and p == 0:
                    dve.wait_ge(const_a, HEAD_MASK)
                for h in range(ACT_HEADS, HC):
                    last = dve.tensor_scalar(k_heads[:, :, :, h, :],
                                             k_t[:, :, :].rearrange("d m (b j) -> d m b j", j=TOK),
                                             head_mask[:, h:h + 1], None, ALU.mult)
                last.then_inc(km_dve_ready, 1)

            def norm1_statistics(p, bank):
                dve.wait_ge(tok_done, p + 1)
                has(dve, hbo_ready, p)
                has(dve, ln1_step, LN1_STEPS * p)
                dve.tensor_tensor(h_tok[:, :], bank[:, 0:D], b_tok, ALU.add).then_inc(h_ready, 1)
                dve.wait_ge(h_ready, p + 1)
                dve.bn_stats(ln1_bn[:, :], h_tok[:, :]).then_inc(ln1_step, 1)
                dve.wait_ge(ln1_step, LN1_STEPS * p + 1)
                settled(dve)
                dve.bn_aggr(ln1_mv[:, :], ln1_bn[:, :]).then_inc(ln1_step, 1)
                dve.wait_ge(ln1_step, LN1_STEPS * p + 2)
                dve.tensor_scalar(ln1_rstd[:, 0:1], ln1_mv[:, 1:2], LN_EPS, None, ALU.add).then_inc(ln1_step, 1)

            def norm1(p):
                dve.wait_ge(ln1_step, LN1_STEPS * p + 4)
                has(dve, ln1t_done, p)
                dve.tensor_scalar(ln1[:, :], h_tok[:, :], ln1_mv[:, 0:1], ln1_rstd[:, 1:2],
                                  ALU.subtract, ALU.mult).then_inc(ln1_step, 1)

            def largest_logits(p):
                dve.wait_ge(ll_done, p + 1)
                has(dve, cexp_ready, p)
                has(dve, dexp_ready, p)
                dve.tensor_reduce(c_max[:, :], kl_ps[:, 0:NS], AX.X, ALU.max, negate=True).then_inc(cmax_ready, 1)
                dve.tensor_reduce(d_max[:, :], kl_ps[0:64, 64:64 + 129], AX.X, ALU.max, negate=True)\
                   .then_inc(dmax_ready, 1)

            def normalise_context(p):
                dve.wait_ge(pv_done, p + 1)
                o = o_ps[:, 0:HP * VW].rearrange("p (i w) -> p i w", w=VW)
                dve.reciprocal(p_inv[:, :].rearrange("p (i e) -> p i e", e=2), o[:, :, 2 * HD:VW])\
                   .then_inc(pinv_ready, 1)
                dve.wait_ge(pinv_ready, p + 1)
                has(dve, ot_done, p)
                dve.tensor_tensor(
                    ctx_n[:, :].rearrange("p (i e d) -> p i e d", e=2, d=HD),
                    o[:, :, 0:2 * HD].rearrange("p i (e d) -> p i e d", e=2),
                    p_inv[:, :].rearrange("p (i e) -> p i e", e=2).unsqueeze(3).to_broadcast([128, HP, 2, HD]),
                    ALU.mult).then_inc(ctx_ready, 1)

            def routing_weights(p):
                dve.wait_ge(cexp_ready, p + 1)
                dve.reciprocal(c_inv[:, :], c_sum[:, :]).then_inc(cinv_ready, 1)
                dve.wait_ge(dexp_ready, p + 1)
                dve.reciprocal(d_inv[:, :], d_sum[:, :]).then_inc(dinv_ready, 1)
                dve.wait_ge(cinv_ready, p + 1)
                has(dve, dc_done, p)
                has(dve, dcls_ready, p)
                for b in range(2):
                    rows = slice(64 * b, 64 * b + 64)
                    last = dve.tensor_scalar(comb[rows, :, b, :], c_exp[rows].unsqueeze(1).to_broadcast([64, 2, NS]),
                                             c_inv[rows, 0:1], None, ALU.mult)
                last.then_inc(comb_ready, 1)
                dve.wait_ge(dinv_ready, p + 1)
                dve.tensor_scalar(disp[:, :], d_exp[:, :], d_inv[:, 0:1], None, ALU.mult).then_inc(disp_ready, 1)

            def spread_values(p):
                dve.wait_ge(v_done, p + 1)
                has(dve, pv_done, p)
                for b in range(2):
                    rows = slice(64 * b, 64 * b + 64)
                    for e in range(2):
                        head = lambda x: x[rows].rearrange("p (i e d) -> p e i d", e=2, d=HD)[:, e]
                        last = dve.tensor_tensor(v_pairs[64 * e:64 * e + 64, b, :, HD * e:HD * e + HD],
                                                 head(vm_ps[:, 0:D]), head(b_v), ALU.add)
                last.then_inc(v_ready, 1)

            def slot(t):
                early = isinstance(t, int)
                largest_scores(t)
                residual_and_variance(t - 1)
                norm2(t - 1, xn, t - 1)
                if early and t == 1:
                    slot_directions()
                spread_keys(t + 1, early)
                norm1_statistics(t + 2, vm_ps)
                largest_logits(t - 1)
                norm1(t + 2)
                routing_weights(t - 1)
                normalise_context(t)
                spread_values(t + 1)

            def slot_biases(c):
                dve.wait_ge(ys_done, c + 1)
                dve.tensor_tensor(y_slots[:, c, :], ys_bank[c][:, 0:D], b_up, ALU.add).then_inc(ys_ready, 1)

            def token_residual(p):
                dve.wait_ge(y_done, p + 1)
                dve.tensor_tensor(h_all[:, p, :], y_bank[p % 3][:, 0:D], h_all[:, p, :], ALU.add).then_inc(y_ready, 1)

            dve.wait_ge(in_a, 16)
            norm1_statistics(0, tok_first_ps)
            cls_statistics()
            norm1(0)
            cls_norm()
            norm1_statistics(1, tok_second_ps)
            norm1(1)
            cls_value()
            spread_keys(0, True)
            spread_values(0)
            slot_squares()
            largest_scores(0)
            cls_output()
            spread_keys(1, True)
            norm1_statistics(2, vm_ps)
            normalise_context(0)
            cls_norm2()
            norm1(2)
            spread_values(1)

            all_slots(dve, slot)

            largest_scores(PAIRS - 2)
            residual_and_variance(PAIRS - 3)
            norm2(PAIRS - 3, xn, PAIRS - 3)
            spread_keys(PAIRS - 1, False)
            normalise_context(PAIRS - 2)
            spread_values(PAIRS - 1)

            largest_scores(PAIRS - 1)
            largest_logits(PAIRS - 3)
            residual_and_variance(PAIRS - 2)
            routing_weights(PAIRS - 3)
            norm2(PAIRS - 2, xn_last, 0)
            cls_largest_logit()
            normalise_context(PAIRS - 1)
            cls_weights()
            largest_logits(PAIRS - 2)
            residual_and_variance(PAIRS - 1)
            routing_weights(PAIRS - 2)
            cls_rows()
            norm2(PAIRS - 1, xn, PAIRS - 2)
            dve.wait_ge(xnt_done, PAIRS)
            dve.wait_ge(ll_done, PAIRS - 1)
            dve.tensor_copy(xn_t[:, :, 0:128],
                            last_norm2_ps[0:DC, 0:256].rearrange("p (k r) -> p k r", k=KC)).then_inc(xnt_ready, 1)

            largest_logits(PAIRS - 1)
            routing_weights(PAIRS - 1)
            slot_biases(0)
            dve.wait_ge(dc_done, PAIRS)
            dve.wait_ge(xx_done, PAIRS - 1)
            dve.tensor_copy(disp_t[:, :], qx_ps[:, 0:64]).then_inc(dispt_ready, 1)
            slot_biases(1)
            slot_biases(2)
            for p in range(EARLY_IMAGES // 2):
                token_residual(p)

            slot_biases(GROUPS - 1)
            for p in range(EARLY_IMAGES // 2, PAIRS):
                token_residual(p)
            dve.wait_ge(yc_done, 1)
            dve.tensor_tensor(cls_out[:, :], yc_ps[0:B, 0:D], cls_h[0:B, :], ALU.add).then_inc(yc_ready, 1)

        @block.scalar
        def _(act):
            for i, part in enumerate(PC_PARTS):
                act.dma_start(xt_first[:, part, :], xt[0, :, part, :]).then_inc(in_first[i], 16)
            act.dma_start(xt_next[:, :, :], xt[1]).then_inc(in_next, 16)
            act.dma_start(pd[:, :], pack_d).then_inc(in_d, 16)

            def load_table(function, into):
                act.wait_ge(idle_ready, 1)
                act.activation(table[:, into:into + 1], table[:, 0:1], function)

            def halves_of(ps, n):
                return ps[0:DC, 0:2 * n].rearrange("p (k r) -> p k r", k=KC)

            def exponentials(p):
                has(act, ptb_done, p)
                for m in range(KC):
                    heads = slice(m * HC, (m + 1) * HC)
                    act.wait_ge(ssub_ready, KC * p + m + 1)
                    last = act.activation(probs[:, heads, :], s_sub[:, heads, 1:TOK], ACT.Exp, scale=SM_SCALE)
                    if m == KC - 1:
                        last = act.activation(probs_cls[:, :], s_sub[:, :, 0], ACT.Exp, scale=SM_SCALE)
                    last.then_inc(probs_ready, 1)

            def queries(p):
                act.wait_ge(qk_done, p + 1)
                has(act, s_done, KC * p)
                for m in range(KC):
                    last = act.activation(q_t[:, m, :], qx_ps[0:DC, m * 128:(m + 1) * 128], ACT.Identity,
                                          bias=b_q[0:DC, m:m + 1])
                last.then_inc(q_ready, 1)

            def keys(p):
                has(act, km_dve_ready, p)
                for m in range(KC):
                    last = act.activation(k_t[:, m, :], kl_ps[0:DC, m * 2 * TOK:(m + 1) * 2 * TOK], ACT.Identity,
                                          bias=b_k[0:DC, m:m + 1])
                last.then_inc(k_ready, 1)

            def spread_keys(p, early):
                if early and p == 0:
                    act.wait_ge(const_a, HEAD_MASK)
                act.wait_ge(k_ready, p + 1)
                for h in range(ACT_HEADS):
                    last = act.activation(k_heads[:, :, :, h, :],
                                          k_t[:, :, :].rearrange("d m (b j) -> d m b j", j=TOK), ACT.Copy,
                                          scale=head_mask[:, h:h + 1])
                last.then_inc(km_act_ready, 1)

            def turned_norm2(p, bank):
                act.wait_ge(xnt_done, p + 1)
                has(act, ll_done, p)
                act.activation(xn_t[:, :, 0:128], halves_of(bank, 128), ACT.Copy).then_inc(xnt_ready, 1)

            def turned_probs(p):
                act.wait_ge(pta_done, p + 1)
                has(act, pv_done, p)
                turned = pt_ps[:, :, 0:HPC * 128].rearrange("p m (i q) -> p m i q", i=HPC)
                act.activation(probs_t[:, 0:HPC, :], turned[:, 0], ACT.Copy).then_inc(pta_ready, 1)
                act.wait_ge(ptb_done, p + 1)
                act.activation(probs_cls_t[:, :], pt_ps[0:HEADS, 1, HPC * 128:(HPC + 1) * 128], ACT.Copy)
                act.activation(probs_t[:, HPC:HP, :], turned[:, 1], ACT.Copy).then_inc(ptb_ready, 1)

            def routing(p):
                act.wait_ge(cmax_ready, p + 1)
                act.wait_ge(dmax_ready, p + 1)
                has(act, comb_ready, p)
                act.activation(c_exp[:, :], kl_ps[:, 0:NS], ACT.Exp, bias=c_max[:, 0:1],
                               accum_out=c_sum[:, 0:1]).then_inc(cexp_ready, 1)
                has(act, disp_ready, p)
                act.activation(d_exp[:, :], kl_ps[0:64, 64:64 + 129], ACT.Exp, bias=d_max[:, 0:1],
                               accum_out=d_sum[:, 0:1]).then_inc(dexp_ready, 1)

            def turned_weights(p):
                act.wait_ge(dc_done, p + 1)
                has(act, xx_done, p)
                if isinstance(p, int) and p == PAIRS - 1:
                    act.wait_ge(dispt_ready, PAIRS)
                else:
                    act.activation(disp_t[:, :], qx_ps[:, 0:64], ACT.Copy).then_inc(dispt_ready, 1)
                act.activation(comb_t[:, p, :], qx_ps[:, 128:256], ACT.Copy).then_inc(combt_ready, 1)

            def turned_context(p, bank):
                act.wait_ge(ot_done, p + 1)
                has(act, wo_done, p)
                act.activation(ctx_t[:, :, :], halves_of(bank, 128), ACT.Copy).then_inc(ctxt_ready, 1)

            def turned_norm1(p):
                act.wait_ge(ln1t_done, p + 1)
                has(act, v_done, p)
                for k in range(KC):
                    last = act.activation(ln1_t[:, k, :, 1:TOK],
                                          o_ps[0:DC, k * 128:(k + 1) * 128].rearrange("p (b r) -> p b r", b=2),
                                          ACT.Copy)
                last.then_inc(ln1t_ready, 1)

            def slot_inputs(p):
                act.wait_ge(xx_done, p + 1)
                act.activation(slots_t[:, :, bass.ds(2 * p, 2), :].rearrange("d k b s -> d k (b s)"),
                               halves_of(vm_ps, 64), ACT.Copy).then_inc(slots_ready, 1)

            def slot(t):
                exponentials(t)
                queries(t + 1)
                keys(t + 1)
                spread_keys(t + 1, False)
                turned_norm2(t - 1, qx_ps)
                turned_probs(t)
                routing(t - 1)
                turned_weights(t - 1)
                turned_context(t, kl_ps)
                turned_norm1(t + 2)
                slot_inputs(t - 1)

            def hidden_units(images):
                for n in range(EXPERTS):
                    g, j = divmod(n, 4)
                    rows = slice(32 * j, 32 * j + 32)
                    at = g * 64 + images.start * SLOTS
                    act.activation(hidden[rows, g, images.start:images.stop, n, :],
                                   hid_ps[rows, at:at + len(images) * SLOTS].rearrange("p (b s) -> p b s", s=SLOTS),
                                   ACT.Gelu, bias=b_down[rows, g:g + 1]).then_inc(hid_ready, 1)

            turned_norm1(0)
            act.wait_ge(cls_step, CLS["ln_turned"])
            act.activation(ln1_t[:, :, :, 0], halves_of(cls_ps, 64)[:, :, 0:2], ACT.Copy)
            act.activation(cls_ln_t[:, :, :], halves_of(cls_ps, 64), ACT.Copy).then_inc(cls_step, 1)
            queries(0)
            keys(0)
            turned_norm1(1)
            spread_keys(0, True)
            act.wait_ge(cls_step, CLS["v_turned"])
            act.activation(cls_v_t[:, :, :], halves_of(cls_ps, 64), ACT.Copy).then_inc(cls_step, 1)
            queries(1)
            keys(1)
            exponentials(0)
            turned_probs(0)
            spread_keys(1, True)
            turned_context(0, kl_ps)
            act.wait_ge(cls_step, CLS["xn_turned"])
            act.activation(cls_xn_t[:, :, :], halves_of(qx_ps, 64), ACT.Copy).then_inc(cls_step, 1)
            act.activation(xn_t[:, :, 128:129], halves_of(qx_ps, 64)[:, :, 0:1], ACT.Copy).then_inc(cls_xn_col, 1)
            turned_norm1(2)

            all_slots(act, slot)

            exponentials(PAIRS - 2)
            queries(PAIRS - 1)
            turned_probs(PAIRS - 2)
            keys(PAIRS - 1)
            turned_norm2(PAIRS - 3, qx_ps)
            spread_keys(PAIRS - 1, False)
            turned_context(PAIRS - 2, last_context_ps)

            exponentials(PAIRS - 1)
            routing(PAIRS - 3)
            turned_probs(PAIRS - 1)
            turned_weights(PAIRS - 3)
            turned_norm2(PAIRS - 2, last_norm2_ps)
            act.wait_ge(cls_step, CLS["max"])
            act.activation(cc_exp[:, :], cls_end_ps[0:64, 0:NS], ACT.Exp, bias=cc_max[:, 0:1],
                           accum_out=cc_sum[:, 0:1]).then_inc(cls_step, 1)
            turned_context(PAIRS - 1, last_context_ps)
            routing(PAIRS - 2)
            slot_inputs(PAIRS - 3)
            load_table(ACT.Gelu, 1)
            act.wait_ge(hid_done, 1)
            act.wait_ge(hidden_zero, 1)
            hidden_units(range(0, EARLY_IMAGES))

            turned_weights(PAIRS - 2)
            load_table(ACT.Exp, 2)
            routing(PAIRS - 1)
            slot_inputs(PAIRS - 2)
            load_table(ACT.Gelu, 3)
            turned_weights(PAIRS - 1)
            slot_inputs(PAIRS - 1)

            act.wait_ge(hid_done, 2)
            hidden_units(range(EARLY_IMAGES, B))
            act.wait_ge(y_ready, PAIRS - 1)
            act.dma_start(out_tok[:, PAIRS - 2, :], h_all[:, PAIRS - 2, :]).then_inc(out_act, 16)
            act.wait_ge(out_act, 16)


def _packed(np, fields, arrays, rows):
    got = np.zeros((rows, width(fields)), np.float32)
    at = 0
    for name, n in fields:
        a = arrays[name]
        got[:a.shape[0], at:at + n] = a.reshape(a.shape[0], n)
        at += n
    return got


def kernel(**inputs):
    import numpy as np
    import concourse.bacc as bacc
    from concourse.bass_utils import run_bass_kernel_spmd

    a = {k.removeprefix("L0_"): np.asarray(v) for k, v in inputs.items()}
    side = 8
    x = a["x"].reshape(PAIRS, 2, side, 16, side, 16, 3).transpose(0, 3, 5, 6, 1, 2, 4)
    x = x.reshape(PAIRS, PC, 128, 128).transpose(0, 2, 1, 3)
    wt = a["tok_W"].reshape(PC, 128, D).transpose(1, 0, 2)

    def rows(v, n=128):
        return np.broadcast_to(v.reshape(1, -1), (n, v.size))

    def chunks(w):
        return w.reshape(KC, DC, -1).transpose(1, 0, 2)

    def heads(w):
        return chunks(w.transpose(1, 0, 2).reshape(D, D))

    wdown = np.zeros((DC, KC, EXPERTS, QW), np.float32)
    wdown[:, :, :, :HID] = chunks(a["ffn_W_down"].transpose(1, 0, 2)).reshape(DC, KC, EXPERTS, HID)
    wup = np.zeros((4, QW, NG, D), np.float32)
    wup[:, :HID] = a["ffn_W_up"].reshape(NG, 4, HID, D).transpose(1, 2, 0, 3)
    bdown = np.zeros((4, QW, NG), np.float32)
    bdown[:, :HID] = a["ffn_b_down"].reshape(NG, 4, HID).transpose(1, 2, 0)
    bup = np.broadcast_to(a["ffn_b_up"][None, :, None, :], (4, EXPERTS, SLOTS, D)).reshape(128, D)
    pack_a = _packed(np, FIELDS_A, {
        "cls": rows(a["cls_tok"]), "btok": rows(a["tok_b"]),
        "bq": a["attn_bq"].reshape(KC, DC).T, "bk": a["attn_bk"].reshape(KC, DC).T,
        "scale": rows(a["ffn_scale"])}, 128)
    pack_d = _packed(np, FIELDS_D, {"bo": rows(a["attn_bo"]), "bv": rows(a["attn_bv"])}, 128)
    pack_b = _packed(np, FIELDS_B, {
        "wq": heads(a["attn_Wq"]), "wk": heads(a["attn_Wk"]), "wv": heads(a["attn_Wv"])}, DC)
    pack_c = _packed(np, FIELDS_C, {
        "wo": chunks(a["attn_Wo"]), "slots": chunks(a["ffn_slot_params"].reshape(D, NS)), "wdown": wdown,
        "wup": wup.reshape(128, NG * D), "bdown": bdown.reshape(128, NG), "bup": bup}, 128)

    nc = bacc.Bacc("TRN2", target_bir_lowering=False, num_devices=1)
    arrays, args = {}, []
    for name, v in (("xt", x), ("wtok", wt), ("pack_a", pack_a), ("pack_b", pack_b), ("pack_d", pack_d), ("pack_c", pack_c)):
        arrays[name] = np.ascontiguousarray(v)
        args.append(nc.dram_tensor(name, arrays[name].shape, F32, kind="ExternalInput").ap())
    args.append(nc.dram_tensor("out_tok", (128, PAIRS, D), F32, kind="ExternalOutput").ap())
    args.append(nc.dram_tensor("out_cls", (B, D), F32, kind="ExternalOutput").ap())
    vit_tower_kernel(nc, *args)
    r = run_bass_kernel_spmd(nc, [arrays], core_ids=[0])
    out = np.empty((B, TOK, D), np.float32)
    out[:, 0] = r.results[0]["out_cls"]
    out[:, 1:] = r.results[0]["out_tok"].transpose(1, 0, 2).reshape(B, NPATCH, D)
    return out
```
